# Optimizing a Trainium2 kernel written in Bass

```python
import numpy as np
import jax
import jax.numpy as jnp

def _softmax(x, axis=-1):
    return jax.nn.softmax(x, axis=axis)

def _gelu(x):
    return jax.nn.gelu(x, approximate=True)

def _silu(x):
    return jax.nn.silu(x)

def _sigmoid(x):
    return jax.nn.sigmoid(x)

def _layernorm(x, axis=-1, eps=1e-05):
    m = jnp.mean(x, axis=axis, keepdims=True)
    v = jnp.var(x, axis=axis, keepdims=True)
    return (x - m) / jnp.sqrt(v + eps)

def _scatter_add(tgt, idx, src, axis=0):
    return tgt.at[idx].add(src)

def _segment_sum(src, seg, n):
    return jax.ops.segment_sum(src, seg, n)
kernel_name = 'mk_cond_resid_d1_seqx_r4_6250b3'

def setup_inputs(seed: int=0):
    np.random.seed(seed)
    _w = jnp.asarray

    def _rec_inputs():
        import jax
        import jax.numpy as jnp
        _rk = jax.random.key(seed)
        x = -0.0003929 + 0.9999 * jax.random.normal(jax.random.fold_in(_rk, 1), (8, 256, 256), jnp.float32)
        _lenS = 256 - jax.random.randint(jax.random.fold_in(_rk, 7), (8,), 0, max(1, 256 // 4) + 1, jnp.int32)
        _lenS2 = 256 - jax.random.randint(jax.random.fold_in(_rk, 8), (8,), 0, max(1, 256 // 4) + 1, jnp.int32)
        itok_B_0_7 = jax.random.randint(jax.random.fold_in(_rk, 11), (8,), 0, 8, jnp.int32)
        return (x, itok_B_0_7)
    x, itok_B_0_7 = _rec_inputs()

    def _L0_cond_setup():
        import jax, jax.numpy as jnp
        import numpy as np
        B, S, D, F = (32, 128, 256, 1024)
        R_COMMON, R_DOMAIN, E = (16, 16, 8)
        ALPHA = 2.0

        def _expert_lora(x, expert_ids, Wa, Wb):
            Ab = Wa[expert_ids]
            Bb = Wb[expert_ids]
            low = jnp.einsum('bsd,brd->bsr', x, Ab)
            return ALPHA * jnp.einsum('bsr,bor->bso', low, Bb)
        key = jax.random.key(seed)
        ks = jax.random.split(key, 12)
        sd = lambda k, shape: jax.random.normal(k, shape, dtype=jnp.float32) * (1.0 / np.sqrt(shape[-1]))
        return {'hidden_states': jax.random.normal(ks[0], (B, S, D), dtype=jnp.float32), 'expert_ids': jax.random.randint(ks[1], (B,), 0, E, dtype=jnp.int32), 'wi': sd(ks[2], (F, D)), 'wo': sd(ks[3], (D, F)), 'common_wi_a': sd(ks[4], (R_COMMON, D)), 'common_wi_b': sd(ks[5], (F, R_COMMON)), 'common_wo_a': sd(ks[6], (R_COMMON, F)), 'common_wo_b': sd(ks[7], (D, R_COMMON)), 'experts_wi_a': sd(ks[8], (E, R_DOMAIN, D)), 'experts_wi_b': sd(ks[9], (F, R_DOMAIN)) * jnp.ones((E, 1, 1)) * 0.0 + sd(ks[9], (E, F, R_DOMAIN)), 'experts_wo_a': sd(ks[10], (E, R_DOMAIN, F)), 'experts_wo_b': sd(ks[11], (E, D, R_DOMAIN))}
    _L0_cond_all = _L0_cond_setup()
    _L0_cond_in = {k: v for k, v in _L0_cond_all.items() if k in ('wi', 'wo', 'common_wi_a', 'common_wi_b', 'common_wo_a', 'common_wo_b', 'experts_wi_a', 'experts_wi_b', 'experts_wo_a', 'experts_wo_b')}
    del _L0_cond_all
    return {'x': x, 'itok_B_0_7': itok_B_0_7, 'L0_cond_wi': _L0_cond_in['wi'], 'L0_cond_wo': _L0_cond_in['wo'], 'L0_cond_common_wi_a': _L0_cond_in['common_wi_a'], 'L0_cond_common_wi_b': _L0_cond_in['common_wi_b'], 'L0_cond_common_wo_a': _L0_cond_in['common_wo_a'], 'L0_cond_common_wo_b': _L0_cond_in['common_wo_b'], 'L0_cond_experts_wi_a': _L0_cond_in['experts_wi_a'], 'L0_cond_experts_wi_b': _L0_cond_in['experts_wi_b'], 'L0_cond_experts_wo_a': _L0_cond_in['experts_wo_a'], 'L0_cond_experts_wo_b': _L0_cond_in['experts_wo_b']}

def reference(x, itok_B_0_7, L0_cond_wi, L0_cond_wo, L0_cond_common_wi_a, L0_cond_common_wi_b, L0_cond_common_wo_a, L0_cond_common_wo_b, L0_cond_experts_wi_a, L0_cond_experts_wi_b, L0_cond_experts_wo_a, L0_cond_experts_wo_b):
    import jax
    import jax.numpy as jnp

    def _L0_cond_ref(hidden_states, expert_ids, wi, wo, common_wi_a, common_wi_b, common_wo_a, common_wo_b, experts_wi_a, experts_wi_b, experts_wo_a, experts_wo_b):
        import jax, jax.numpy as jnp
        import numpy as np
        B, S, D, F = (32, 128, 256, 1024)
        R_COMMON, R_DOMAIN, E = (16, 16, 8)
        ALPHA = 2.0

        def _expert_lora(x, expert_ids, Wa, Wb):
            Ab = Wa[expert_ids]
            Bb = Wb[expert_ids]
            low = jnp.einsum('bsd,brd->bsr', x, Ab)
            return ALPHA * jnp.einsum('bsr,bor->bso', low, Bb)
        x = hidden_states
        hidden_i = jnp.einsum('bsd,fd->bsf', x, wi)
        hidden_i += ALPHA * jnp.einsum('bsr,fr->bsf', jnp.einsum('bsd,rd->bsr', x, common_wi_a), common_wi_b)
        hidden_i += _expert_lora(x, expert_ids, experts_wi_a, experts_wi_b)
        hidden_i = jax.nn.relu(hidden_i)
        hidden_o = jnp.einsum('bsf,df->bsd', hidden_i, wo)
        hidden_o += ALPHA * jnp.einsum('bsr,dr->bsd', jnp.einsum('bsf,rf->bsr', hidden_i, common_wo_a), common_wo_b)
        hidden_o += _expert_lora(hidden_i, expert_ids, experts_wo_a, experts_wo_b)
        return hidden_o
    x = x + _L0_cond_ref(x, itok_B_0_7, L0_cond_wi, L0_cond_wo, L0_cond_common_wi_a, L0_cond_common_wi_b, L0_cond_common_wo_a, L0_cond_common_wo_b, L0_cond_experts_wi_a, L0_cond_experts_wi_b, L0_cond_experts_wo_a, L0_cond_experts_wo_b)
    return x

_drawn_inputs = setup_inputs


def setup_inputs(seed=0):
    import zlib

    import numpy as np

    out = dict(_drawn_inputs(seed))
    spreads = {}
    factors = {}
    for name, (base, spread) in spreads.items():
        noise = np.random.default_rng([zlib.crc32(name.encode()), seed]).standard_normal(out[name].shape)
        drawn = base * np.exp(spread * noise) if base else spread * noise
        out[name] = jnp.asarray(drawn.astype(out[name].dtype))
    for name, factor in factors.items():
        out[name] = (out[name] * factor).astype(out[name].dtype)
    return out
```

```python
from contextlib import ExitStack

import concourse.bass as bass
from concourse import mybir

F32 = mybir.dt.float32
F32R = mybir.dt.float32r
I32 = mybir.dt.int32
ALU = mybir.AluOpType
ACT = mybir.ActivationFunctionType
HI, LO = 0, 1
ALPHA = 2.0


def conditional_ffn(nc, x, ids, wi, wo, c_wi_a, c_wi_b, c_wo_a, c_wo_b, e_wi_a, e_wi_b, e_wo_a, e_wo_b, out):
    P = 128
    B, S, D = x.shape
    F = wi.shape[0]
    E, R, _ = e_wi_a.shape
    KD = D // P
    MF = F // P
    PAIR = 2
    T = PAIR * S
    TT = T // P
    STEPS = B // PAIR
    ER = E * R
    BLK = 2 * R
    KL = 3 * BLK
    WIN = D + BLK
    WC = R + D + R + R
    BANK = 512
    PB = BANK // P
    assert ER == P and T == BANK and STEPS * PAIR == B and 8 * R == P and 2 * R == 32

    B_PART = [HI, LO, HI, HI]
    LOW_LO_BLOCK = 2
    BO_PART = [HI, LO, HI]
    E_ROW = [0, R]
    C_ROW = [R, 0]
    WIN_AT = [0, R]
    OUT_AT = [R, 0]

    xv = x.rearrange("b s d -> (b s) d").rearrange("(q t p) d -> q p t d", p=P, t=TT)
    ov = out.rearrange("b s d -> (b s) d").rearrange("(q t p) d -> q t p d", p=P, t=TT)

    bi_parts = nc.dram_tensor("bi_parts", [2, ER, F], F32, kind="Internal").ap()
    bo_parts = nc.dram_tensor("bo_parts", [2, ER, D], F32, kind="Internal").ap()

    with ExitStack() as ctx:
        def sb(name, shape, dt=F32):
            return ctx.enter_context(nc.sbuf_tensor(name, shape, dt))

        def sem(name):
            return ctx.enter_context(nc.semaphore(name))

        bank_h = [ctx.enter_context(nc.psum_tensor(f"bank_h{i}", [P, BANK], F32)) for i in range(4)]
        bank_o = [ctx.enter_context(nc.psum_tensor(f"bank_o{i}", [P, BANK], F32)) for i in range(2)]
        bank_x = [ctx.enter_context(nc.psum_tensor(f"bank_x{i}", [P, BANK], F32)) for i in range(2)]
        out_bank = [bank_h[0], bank_h[1], bank_o[0], bank_o[1]]
        tl_bank = [bank_h[2], bank_h[3], bank_h[2], bank_h[3]]

        ident = sb("ident", [P, P])
        idt = sb("idt", [1, B], I32)
        wi_nat = sb("wi_nat", [P, MF, D])
        wo_nat = sb("wo_nat", [P, KD, F])
        ai_nat = sb("ai_nat", [ER, D])
        aic_nat = sb("aic_nat", [R, D])
        ao_nat = sb("ao_nat", [ER, F])
        aoc_nat = sb("aoc_nat", [R, F])
        bi_raw = sb("bi_raw", [P, E, MF * R])
        bi_nat = sb("bi_nat", [P, MF, ER])
        bic_nat = sb("bic_nat", [P, MF, R])
        bo_raw = sb("bo_raw", [P, E, KD * R])
        bo_nat = sb("bo_nat", [P, KD, ER])
        boc_nat = sb("boc_nat", [P, KD, R])
        wiT = [sb(f"wiT{s}", [P, KD, F], F32R) for s in (HI, LO)]
        aiT = [sb(f"aiT{s}", [P, KD * ER + KD * R], F32R) for s in (HI, LO)]
        aoT = [sb(f"aoT{s}", [P, MF, ER], F32R) for s in (HI, LO)]
        biT = [sb(f"biT{s}", [ER, F], F32R) for s in (HI, LO)]
        bicT = [sb(f"bicT{s}", [R, F], F32R) for s in (HI, LO)]
        boT = [sb(f"boT{s}", [ER, D], F32R) for s in (HI, LO)]
        bocT = [sb(f"bocT{s}", [R, D], F32R) for s in (HI, LO)]
        wcat = [sb(f"wcat{s}", [P, MF, WC], F32R) for s in (HI, LO)]
        ai_stack = sb("ai_stack", [P, PAIR, KD, P], F32R)
        bi_stack = sb("bi_stack", [P, PAIR, F], F32R)
        bo_stack = sb("bo_stack", [KL, PAIR, D], F32R)
        x_nat = sb("x_nat", [P, TT, D])
        x_res = sb("x_res", [P, TT, D])
        xT = [sb(f"xT{s}", [P, KD, T], F32R) for s in (HI, LO)]
        low_stack = sb("low_stack", [P, T], F32R)
        hid = [sb(f"hid{s}", [P, MF, T], F32R) for s in (HI, LO)]
        lo_sb = sb("lo_sb", [P, 3, 2, R])
        lo_stack = [sb(f"lo_stack{i}", [KL, P], F32R) for i in range(2)]
        o_sb = sb("o_sb", [P, TT, D])

        ids_in, x_in = sem("ids_in"), sem("x_in")
        wi_in = [sem(f"wi_in{i}") for i in range(2)]
        wo_in, ai_in, ao_in, bi_in, bo_in = (sem(n) for n in ("wo_in", "ai_in", "ao_in", "bi_in", "bo_in"))
        ident_zero, ident_ready = sem("ident_zero"), sem("ident_ready")
        b_nat_ready = sem("b_nat_ready")
        wt_done, wt_hi, wt_lo = sem("wt_done"), sem("wt_hi"), sem("wt_lo")
        common_ready = sem("common_ready")
        parts_out = sem("parts_out")
        ai_ready, ao_ready = sem("ai_ready"), [sem(f"ao_ready{b}") for b in range(PAIR)]
        bi_loaded, bo_loaded = sem("bi_loaded"), [sem(f"bo_loaded{b}") for b in range(PAIR)]
        stack_common = sem("stack_common")
        res_ready = sem("res_ready")
        xt_done, xt_hi, xt_lo = sem("xt_done"), sem("xt_hi"), sem("xt_lo")
        low_done, low_hi, low_lo = sem("low_done"), sem("low_hi"), sem("low_lo")
        up_done, hid_hi, hid_lo = sem("up_done"), sem("hid_hi"), sem("hid_lo")
        main_done, lo_copied = sem("main_done"), sem("lo_copied")
        tl_done, tl_hi, tl_lo = sem("tl_done"), sem("tl_hi"), sem("tl_lo")
        fin_done, added, stored = sem("fin_done"), sem("added"), sem("stored")

        def bank_tiles(bank, tiles):
            return [(bank[0:n, at:at + k], src) for at, n, k, src in tiles]

        def f_scatter(t, n, half):
            return t[0:n, :].rearrange("n (p j) -> n j p", j=MF)[:, half * PB:(half + 1) * PB, :]

        def g_bi(half):
            bank = bank_o[half]
            tiles = [(i * P, ER, P, bi_nat[:, half * PB + i, :]) for i in range(PB)]
            src = bank[:, :].rearrange("n (j p) -> n j p", p=P)
            return dict(tiles=bank_tiles(bank, tiles), wait=[(b_nat_ready, 1)],
                        parts=[(src, f_scatter(biT[HI], ER, half), f_scatter(biT[LO], ER, half))])

        def g_bic(half):
            bank = [bank_o[1], bank_x[1]][half]
            tiles = [(i * P, R, P, bic_nat[:, half * PB + i, :]) for i in range(PB)]
            src = bank[0:R, :].rearrange("n (j p) -> n j p", p=P)
            return dict(tiles=bank_tiles(bank, tiles), wait=[(bi_in, 32)],
                        parts=[(src, f_scatter(bicT[HI], R, half), f_scatter(bicT[LO], R, half))])

        def g_wi(k, half):
            bank = bank_h[half * KD + k]
            tiles = [(i * P, P, P, wi_nat[:, half * PB + i, k * P:(k + 1) * P]) for i in range(PB)]
            to = [wiT[s][:, k, half * BANK:(half + 1) * BANK] for s in (HI, LO)]
            return dict(tiles=bank_tiles(bank, tiles), wait=[(wi_in[half], 16)], parts=[(bank[:, :], *to)])

        def g_ai():
            bank, n = bank_o[0], KD * ER + KD * R
            tiles = [(k * ER, P, ER, ai_nat[:, k * P:(k + 1) * P]) for k in range(KD)]
            tiles += [(KD * ER + k * R, P, R, aic_nat[:, k * P:(k + 1) * P]) for k in range(KD)]
            return dict(tiles=bank_tiles(bank, tiles), wait=[(ai_in, 32)],
                        parts=[(bank[:, 0:n], aiT[HI][:, :], aiT[LO][:, :])])

        def g_bo():
            bank = bank_o[0]
            tiles = [(k * P, ER, P, bo_nat[:, k, :]) for k in range(KD)]
            tiles += [((KD + k) * P, R, P, boc_nat[:, k, :]) for k in range(KD)]
            parts = []
            for at, n, t in ((0, ER, boT), (KD * P, R, bocT)):
                src = bank[0:n, at:at + KD * P].rearrange("n (k p) -> n k p", p=P)
                parts.append((src, *(t[s][:, :].rearrange("n (p k) -> n k p", k=KD) for s in (HI, LO))))
            return dict(tiles=bank_tiles(bank, tiles), wait=[(b_nat_ready, 2), (bo_in, 32)], parts=parts)

        ring = [bank_o[1], bank_x[1], bank_x[0], bank_o[0]]

        def g_wo(i):
            bank = ring[i % 4]
            tiles = [((jj * KD + k) * P, P, P, wo_nat[:, k, (2 * i + jj) * P:(2 * i + jj + 1) * P])
                     for jj in range(2) for k in range(KD)]
            to = [wcat[s][:, 2 * i:2 * i + 2, R:R + D] for s in (HI, LO)]
            return dict(tiles=bank_tiles(bank, tiles), wait=[(wo_in, 16)],
                        parts=[(bank[:, :].rearrange("p (j d) -> p j d", d=D), *to)])

        def g_ao(half):
            bank = ring[half]
            tiles = [(i * ER, P, ER, ao_nat[:, (half * PB + i) * P:(half * PB + i + 1) * P]) for i in range(PB)]
            to = [aoT[s][:, half * PB:(half + 1) * PB, :] for s in (HI, LO)]
            return dict(tiles=bank_tiles(bank, tiles), wait=[(ao_in, 32)],
                        parts=[(bank[:, :].rearrange("p (j n) -> p j n", n=ER), *to)])

        def g_aoc():
            bank = ring[2]
            tiles = [(j * R, P, R, aoc_nat[:, j * P:(j + 1) * P]) for j in range(MF)]
            to = [wcat[s][:, :, R + D:R + D + R] for s in (HI, LO)]
            return dict(tiles=bank_tiles(bank, tiles), wait=[(ao_in, 32)],
                        parts=[(bank[:, 0:MF * R].rearrange("p (j n) -> p j n", n=R), *to)])

        early = [g_bi(0), g_bi(1), g_wi(0, 0), g_wi(1, 0), g_wi(0, 1), g_wi(1, 1), g_ai(), g_bic(0), g_bic(1), g_bo()]
        late = [g_wo(0), g_wo(1), g_wo(2), g_wo(3), g_ao(0), g_ao(1), g_aoc()]
        BEFORE = {6: 1, 7: 2, 8: None, 9: 7}
        BEFORE |= {len(early) + i: n for i, n in enumerate([8, 9, 0, 10, 11, 12, 13])}
        AI_GROUP, BI_GROUP, BIC_GROUP, BO_GROUP = 7, 2, 9, 10
        AO_GROUP, ALL_GROUPS = len(early) + 6, len(early) + len(late)

        block = ctx.enter_context(nc.Block())

        @block.sync
        def _(sp):
            sp.dma_start(idt[:, :], ids.rearrange("(o n) -> o n", o=1)).then_inc(ids_in, 16)
            sp.dma_start(bi_raw[:, :, :], e_wi_b.rearrange("e (p j) r -> p e (j r)", p=P)).then_inc(bi_in, 16)
            sp.dma_start(bic_nat[:, :, :], c_wi_b.rearrange("(p j) r -> p j r", p=P)).then_inc(bi_in, 16)
            sp.dma_start(ai_nat[:, :], e_wi_a.rearrange("e r d -> (e r) d")).then_inc(ai_in, 16)
            sp.dma_start(aic_nat[:, :], c_wi_a).then_inc(ai_in, 16)
            sp.dma_start(bo_raw[:, :, :], e_wo_b.rearrange("e (p k) r -> p e (k r)", p=P)).then_inc(bo_in, 16)
            sp.dma_start(boc_nat[:, :, :], c_wo_b.rearrange("(p k) r -> p k r", p=P)).then_inc(bo_in, 16)
            sp.dma_start(wo_nat[:, :, :], wo.rearrange("(k p) f -> p k f", p=P)).then_inc(wo_in, 16)

            sp.wait_ge(wt_lo, BI_GROUP)
            for s in (HI, LO):
                sp.dma_start(bi_parts[s], biT[s][:, :].bitcast(F32)).then_inc(parts_out, 16)

            def expert_rows(step):
                rows = []
                for b in range(PAIR):
                    e = sp.value_load(idt[0:1, bass.ds(step * PAIR + b, 1)], min_val=0, max_val=E - 1)
                    rows.append(sp.snap(e * R))
                return rows

            def load_bi(rows):
                for b in range(PAIR):
                    for i, s in enumerate(B_PART):
                        sp.dma_start(bi_stack[i * R:(i + 1) * R, b, :].bitcast(F32),
                                     bi_parts[s, bass.ds(rows[b], R), :]).then_inc(bi_loaded, 16)

            def load_bo(rows, b):
                for i, s in enumerate(BO_PART):
                    at = i * BLK + E_ROW[b]
                    sp.dma_start(bo_stack[at:at + R, b, :].bitcast(F32),
                                 bo_parts[s, bass.ds(rows[b], R), :]).then_inc(bo_loaded[b], 16)

            def store(step, t):
                sp.wait_ge(added, step * TT + t + 1)
                sp.dma_start(ov[step, t] if isinstance(step, int) else ov[bass.ds(step, 1), t, :, :].rearrange("o p d -> (o p) d"),
                             o_sb[:, t, :]).then_inc(stored, 16)

            sp.wait_ge(ids_in, 16)
            rows = expert_rows(0)
            sp.wait_ge(parts_out, 32)
            load_bi(rows)
            sp.wait_ge(wt_lo, BIC_GROUP)
            for b in range(PAIR):
                for i, s in enumerate(B_PART):
                    at = (4 + i) * R
                    sp.dma_start(bi_stack[at:at + R, b, :].bitcast(F32),
                                 bicT[s][:, :].bitcast(F32)).then_inc(stack_common, 16)
            sp.wait_ge(wt_lo, BO_GROUP)
            for s in (HI, LO):
                sp.dma_start(bo_parts[s], boT[s][:, :].bitcast(F32)).then_inc(parts_out, 16)
            for b in range(PAIR):
                for i, s in enumerate(BO_PART):
                    at = i * BLK + C_ROW[b]
                    sp.dma_start(bo_stack[at:at + R, b, :].bitcast(F32),
                                 bocT[s][:, :].bitcast(F32)).then_inc(stack_common, 16)
            sp.wait_ge(parts_out, 64)
            for b in range(PAIR):
                load_bo(rows, b)

            with sp.Fori(0, STEPS - 1) as q:
                rows = expert_rows(q + 1)
                sp.wait_ge(res_ready, q + 1)
                sp.wait_ge(xt_done, (q + 1) * KD)
                sp.dma_start(x_nat[:, :, :], xv[bass.ds(q + 1, 1), :, :, :].rearrange("o p t d -> (o p) t d")).then_inc(x_in, 16)
                sp.wait_ge(up_done, (q + 1) * MF)
                load_bi(rows)
                store(q, 0)
                store(q, 1)
                sp.wait_ge(fin_done, q * TT + 2)
                load_bo(rows, 0)
                store(q, 2)
                store(q, 3)
                sp.wait_ge(fin_done, q * TT + 4)
                load_bo(rows, 1)
            for t in range(TT):
                store(STEPS - 1, t)
            sp.wait_ge(stored, STEPS * TT * 16)

        @block.gpsimd
        def _(pool):
            nc.gpsimd.memset(ident[:, :], 0.0).then_inc(ident_zero, 1)
            pool.wait_ge(ident_zero, 1)
            nc.gpsimd.affine_select(out=ident[:, :], in_=ident[:, :], compare_op=ALU.not_equal, fill=1.0, base=0,
                                    pattern=[[-1, P]], channel_multiplier=1).then_inc(ident_ready, 1)

            def spread_ai(b, at, src):
                hi, lo = (src(s).bitcast(F32) for s in (HI, LO))
                nc.gpsimd.tensor_copy(
                    ai_stack[:, b, :, at:at + 3 * R].rearrange("p k (i r) -> p k i r", r=R),
                    hi.unsqueeze(2).broadcast_to([P, KD, 3, R]))
                return nc.gpsimd.tensor_copy(ai_stack[:, b, :, at + 3 * R:at + 4 * R], lo)

            def experts(step):
                return [pool.value_load(idt[0:1, bass.ds(step * PAIR + b, 1)], min_val=0, max_val=E - 1)
                        for b in range(PAIR)]

            def copy_ai(at):
                for b in range(PAIR):
                    last = spread_ai(b, 0, lambda s: aiT[s][:, 0:KD * ER].rearrange("p (k n) -> p k n", k=KD)[
                        :, :, bass.ds(at[b], R)])
                last.then_inc(ai_ready, 1)

            def copy_ao(at, b):
                to = [0, R + D + R][b]
                for s in (HI, LO):
                    last = nc.gpsimd.tensor_copy(wcat[s][:, :, to:to + R], aoT[s][:, :, bass.ds(at[b], R)].bitcast(F32))
                last.then_inc(ao_ready[b], 1)

            pool.wait_ge(ids_in, 16)
            pool.wait_ge(wt_lo, AI_GROUP)
            for b in range(PAIR):
                last = spread_ai(b, 4 * R, lambda s: aiT[s][:, KD * ER:].rearrange("p (k n) -> p k n", k=KD))
            last.then_inc(common_ready, 1)
            at = [pool.snap(e * R) for e in experts(0)]
            copy_ai(at)
            pool.wait_ge(wt_lo, AO_GROUP)
            for b in range(PAIR):
                copy_ao(at, b)
            with pool.Fori(0, STEPS - 1) as q:
                at = [pool.snap(e * R) for e in experts(q + 1)]
                pool.wait_ge(low_done, q + 1)
                copy_ai(at)
                pool.wait_ge(main_done, q * TT + 2)
                copy_ao(at, 0)
                pool.wait_ge(main_done, q * TT + 4)
                copy_ao(at, 1)

        @block.scalar
        def _(act):
            act.dma_start(x_nat[:, :, :], xv[0]).then_inc(x_in, 16)
            for i in range(2):
                j = slice(i * MF // 2, (i + 1) * MF // 2)
                act.dma_start(wi_nat[:, j, :], wi.rearrange("(j p) d -> p j d", p=P)[:, j, :]).then_inc(wi_in[i], 16)
            act.dma_start(ao_nat[:, :], e_wo_a.rearrange("e r f -> (e r) f")).then_inc(ao_in, 16)
            act.dma_start(aoc_nat[:, :], c_wo_a).then_inc(ao_in, 16)

            def weight_hi(n, group):
                act.wait_ge(wt_done, n + 1)
                for src, hi, _ in group["parts"]:
                    last = nc.scalar.copy(hi, src)
                last.then_inc(wt_hi, 1)

            def x_hi(step):
                for k in range(KD):
                    act.wait_ge(xt_done, step * KD + k + 1)
                    nc.scalar.copy(xT[HI][:, k, :], bank_x[k][:, :]).then_inc(xt_hi, 1)

            def lowi_hi(step):
                act.wait_ge(low_done, step + 1)
                nc.scalar.mul(low_stack[:, :], bank_x[0][:, :], ALPHA).then_inc(low_hi, 1)

            def hidden_hi(step, m):
                act.wait_ge(up_done, step * MF + m + 1)
                nc.scalar.activation(hid[HI][:, m, :], bank_h[m % 4][:, :], ACT.Relu).then_inc(hid_hi, 1)

            def low_copy(step, t):
                act.wait_ge(main_done, step * TT + t + 1)
                b = t // (TT // PAIR)
                ranks = out_bank[t][:, 0:WIN].rearrange("p (n r) -> p n r", r=R)
                ranks = ranks[:, 0:WIN // R:WIN // R - 1, :] if b == 0 else ranks[:, WIN // R - 2:, :]
                nc.scalar.copy(lo_sb[:, :, :, :], ranks.unsqueeze(1).broadcast_to([P, 3, 2, R])).then_inc(lo_copied, 1)

            def tl_part(step, t):
                act.wait_ge(tl_done, step * TT + t + 1)
                nc.scalar.mul(lo_stack[t % 2][:, :], tl_bank[t][0:KL, 0:P], ALPHA).then_inc(tl_hi, 1)

            def down(step, more):
                low_copy(step, 0)
                tl_part(step, 0)
                if more:
                    x_hi(step + 1)
                for t in range(1, TT):
                    low_copy(step, t)
                    tl_part(step, t)
                if more:
                    lowi_hi(step + 1)

            for n in range(2):
                weight_hi(n, early[n])
            x_hi(0)
            for n in range(2, len(early)):
                weight_hi(n, early[n])
                if n == AI_GROUP:
                    pass
            lowi_hi(0)
            for m in range(MF):
                hidden_hi(0, m)
                if m < len(late):
                    weight_hi(len(early) + m, late[m])
            with act.Fori(0, STEPS - 1) as q:
                down(q, True)
                for m in range(MF):
                    hidden_hi(q + 1, m)
            down(STEPS - 1, False)

        @block.vector
        def _(dve):
            def lo_part(out_, src, scale, hi):
                op = ALU.max if scale is None else ALU.mult
                return nc.vector.scalar_tensor_tensor(out=out_, in0=src, scalar=0.0 if scale is None else scale,
                                                      in1=hi.bitcast(F32), op0=op, op1=ALU.subtract)

            def weight_lo(n, group):
                dve.wait_ge(wt_hi, n + 1)
                for src, hi, lo in group["parts"]:
                    last = nc.vector.tensor_tensor(lo, src, hi.bitcast(F32), ALU.subtract)
                last.then_inc(wt_lo, 1)

            def x_lo(step):
                for k in range(KD):
                    dve.wait_ge(xt_hi, step * KD + k + 1)
                    nc.vector.tensor_tensor(xT[LO][:, k, :], bank_x[k][:, :], xT[HI][:, k, :].bitcast(F32),
                                            ALU.subtract).then_inc(xt_lo, 1)

            def keep_x(step):
                dve.wait_ge(x_in, (step + 1) * 16)
                if not isinstance(step, int):
                    dve.wait_ge(added, step * TT)
                nc.vector.tensor_copy(x_res[:, :, :], x_nat[:, :, :]).then_inc(res_ready, 1)

            def lowi_lo(step):
                dve.wait_ge(low_hi, step + 1)
                for at in (LOW_LO_BLOCK * R, (4 + LOW_LO_BLOCK) * R):
                    rows = low_stack[at:at + R, :]
                    lo_part(rows, bank_x[0][at:at + R, :], ALPHA, rows).then_inc(low_lo, 1)

            def hidden_lo(step, m):
                dve.wait_ge(hid_hi, step * MF + m + 1)
                lo_part(hid[LO][:, m, :], bank_h[m % 4][:, :], None, hid[HI][:, m, :]).then_inc(hid_lo, 1)

            def tl_lo_part(step, t):
                dve.wait_ge(tl_hi, step * TT + t + 1)
                rows = lo_stack[t % 2][2 * BLK:KL, :]
                lo_part(rows, tl_bank[t][2 * BLK:KL, 0:P], ALPHA, rows).then_inc(tl_lo, 1)

            def add(step, t):
                b = t // (TT // PAIR)
                dve.wait_ge(fin_done, step * TT + t + 1)
                if t == 0:
                    dve.wait_ge(res_ready, step + 1)
                    dve.wait_ge(stored, step * TT * 16)
                nc.vector.tensor_tensor(o_sb[:, t, :], out_bank[t][:, OUT_AT[b]:OUT_AT[b] + D], x_res[:, t, :],
                                        ALU.add).then_inc(added, 1)

            def down(step, more):
                tl_lo_part(step, 0)
                if more:
                    x_lo(step + 1)
                add(step, 0)
                tl_lo_part(step, 1)
                add(step, 1)
                tl_lo_part(step, 2)
                tl_lo_part(step, 3)
                add(step, 2)
                add(step, 3)
                if more:
                    lowi_lo(step + 1)
                    keep_x(step + 1)

            dve.wait_ge(bi_in, 32)
            nc.vector.tensor_copy(bi_nat[:, :, :].rearrange("p j (e r) -> p j e r", r=R),
                                  bi_raw[:, :, :].rearrange("p e (j r) -> p j e r", r=R)).then_inc(b_nat_ready, 1)
            dve.wait_ge(bo_in, 32)
            nc.vector.tensor_copy(bo_nat[:, :, :].rearrange("p k (e r) -> p k e r", r=R),
                                  bo_raw[:, :, :].rearrange("p e (k r) -> p k e r", r=R)).then_inc(b_nat_ready, 1)
            for n in range(2):
                weight_lo(n, early[n])
            x_lo(0)
            for n in range(2, len(early)):
                weight_lo(n, early[n])
            lowi_lo(0)
            keep_x(0)
            for m in range(MF):
                hidden_lo(0, m)
                if m < len(late):
                    weight_lo(len(early) + m, late[m])
            with dve.Fori(0, STEPS - 1) as q:
                down(q, True)
                for m in range(MF):
                    hidden_lo(q + 1, m)
            down(STEPS - 1, False)

        @block.tensor
        def _(pe):
            def transpose_weights(n, group):
                for s, v in group["wait"]:
                    pe.wait_ge(s, v)
                if BEFORE.get(n):
                    pe.wait_ge(wt_lo, BEFORE[n])
                for dst, src in group["tiles"]:
                    last = nc.tensor.transpose(dst, src, ident[0:src.shape[0], 0:src.shape[0]])
                last.then_inc(wt_done, 1)

            def transpose_x(step):
                pe.wait_ge(x_in, (step + 1) * 16)
                for k in range(KD):
                    for t in range(TT):
                        last = nc.tensor.transpose(bank_x[k][:, t * P:(t + 1) * P], x_nat[:, t, k * P:(k + 1) * P],
                                                   ident[:, :])
                    last.then_inc(xt_done, 1)

            def low_in(step, b):
                if b == 0:
                    pe.wait_ge(xt_lo, (step + 1) * KD)
                    pe.wait_ge(ai_ready, step + 1)
                cols = slice(b * S, (b + 1) * S)
                for k in range(KD):
                    for s in (HI, LO):
                        last = nc.tensor.matmul(bank_x[0][:, cols], ai_stack[:, b, k, :], xT[s][:, k, cols],
                                                start=(k == 0 and s == HI), stop=(k == KD - 1 and s == LO))
                if b == PAIR - 1:
                    last.then_inc(low_done, 1)

            def up_main(step, m):
                if m >= 4:
                    pe.wait_ge(hid_lo, step * MF + m - 3)
                f = slice(m * P, (m + 1) * P)
                for i, (k, sw, sx) in enumerate((k, sw, sx) for k in range(KD)
                                                for sw, sx in ((HI, HI), (HI, LO), (LO, HI))):
                    nc.tensor.matmul(bank_h[m % 4][:, :], wiT[sw][:, k, f], xT[sx][:, k, :], start=(i == 0), stop=False)

            def up_lora(step, m):
                if m == 0:
                    pe.wait_ge(low_lo, (step + 1) * 2)
                    pe.wait_ge(bi_loaded, (step + 1) * PAIR * 4 * 16)
                for b in range(PAIR):
                    cols = slice(b * S, (b + 1) * S)
                    last = nc.tensor.matmul(bank_h[m % 4][:, cols], bi_stack[:, b, m * P:(m + 1) * P],
                                            low_stack[:, cols], start=False, stop=(b == PAIR - 1))
                last.then_inc(up_done, 1)

            def up(step, extra=None):
                for m in range(MF + 1):
                    if m < MF:
                        up_main(step, m)
                    if m > 0:
                        up_lora(step, m - 1)
                    if extra and 0 < m <= len(late):
                        transpose_weights(len(early) + m - 1, late[m - 1])

            def main(step, t):
                b = t // (TT // PAIR)
                tok = slice(t * P, (t + 1) * P)
                win = slice(WIN_AT[b], WIN_AT[b] + WIN)
                if t % (TT // PAIR) == 0:
                    pe.wait_ge(ao_ready[b], step + 1)
                if t == 1:
                    pe.wait_ge(hid_lo, step * MF + 6)
                if t == 2:
                    pe.wait_ge(added, step * TT)
                for m in range(MF):
                    if t == 0:
                        pe.wait_ge(hid_lo, step * MF + max(m + 1, 5))
                    for i, (sh, sw) in enumerate(((HI, HI), (HI, LO), (LO, HI))):
                        last = nc.tensor.matmul(out_bank[t][:, 0:WIN], hid[sh][:, m, tok], wcat[sw][:, m, win],
                                                start=(m == 0 and i == 0), stop=(m == MF - 1 and i == 2))
                last.then_inc(main_done, 1)

            def turn_low(step, t):
                pe.wait_ge(lo_copied, step * TT + t + 1)
                if t < 2:
                    pe.wait_ge(hid_lo, step * MF + 7 + t)
                nc.tensor.transpose(tl_bank[t][0:KL, 0:P], lo_sb[:, :, :, :].rearrange("p i a r -> p (i a r)"),
                                    ident[:, :]).then_inc(tl_done, 1)

            def fin(step, t):
                b = t // (TT // PAIR)
                pe.wait_ge(tl_lo, step * TT + t + 1)
                if t % (TT // PAIR) == 0:
                    pe.wait_ge(bo_loaded[b], (step + 1) * 3 * 16)
                nc.tensor.matmul(out_bank[t][:, OUT_AT[b]:OUT_AT[b] + D], lo_stack[t % 2][:, :], bo_stack[:, b, :],
                                 start=False, stop=True, skip_group_check=True).then_inc(fin_done, 1)

            def down(step, more):
                main(step, 0)
                main(step, 1)
                turn_low(step, 0)
                if more:
                    transpose_x(step + 1)
                main(step, 2)
                fin(step, 0)
                turn_low(step, 1)
                main(step, 3)
                fin(step, 1)
                turn_low(step, 2)
                if more:
                    low_in(step + 1, 0)
                turn_low(step, 3)
                fin(step, 2)
                if more:
                    low_in(step + 1, 1)
                fin(step, 3)

            pe.wait_ge(ident_ready, 1)
            for n in range(2):
                transpose_weights(n, early[n])
            transpose_x(0)
            for n in range(2, len(early)):
                if n == 8:
                    pe.wait_ge(xt_lo, KD)
                transpose_weights(n, early[n])
            pe.wait_ge(common_ready, 1)
            low_in(0, 0)
            low_in(0, 1)
            pe.wait_ge(wt_lo, 6)
            pe.wait_ge(stack_common, (4 * PAIR + 3 * PAIR) * 16)
            up(0, True)
            pe.wait_ge(wt_lo, ALL_GROUPS)
            with pe.Fori(0, STEPS - 1) as q:
                down(q, True)
                up(q + 1)
            down(STEPS - 1, False)


_INS = ["x", "itok_B_0_7", "L0_cond_wi", "L0_cond_wo", "L0_cond_common_wi_a", "L0_cond_common_wi_b",
        "L0_cond_common_wo_a", "L0_cond_common_wo_b", "L0_cond_experts_wi_a", "L0_cond_experts_wi_b",
        "L0_cond_experts_wo_a", "L0_cond_experts_wo_b"]


def kernel(**inputs):
    import numpy as np
    import concourse.bacc as bacc
    from concourse.bass_utils import run_bass_kernel_spmd

    nc = bacc.Bacc("TRN2", target_bir_lowering=False, num_devices=1)
    arrays, args = {}, []
    for name in _INS:
        a = np.ascontiguousarray(inputs[name])
        arrays[f"in_{name}"] = a
        args.append(nc.dram_tensor(f"in_{name}", a.shape, mybir.dt.from_np(a.dtype), kind="ExternalInput").ap())
    args.append(nc.dram_tensor("out_0", inputs["x"].shape, F32, kind="ExternalOutput").ap())
    conditional_ffn(nc, *args)
    result = run_bass_kernel_spmd(nc, [arrays], core_ids=[0])
    return result.results[0]["out_0"]
```

```python
from contextlib import ExitStack

import concourse.bass as bass
from concourse import mybir

F32 = mybir.dt.float32
F32R = mybir.dt.float32r
I32 = mybir.dt.int32
ALU = mybir.AluOpType
ACT = mybir.ActivationFunctionType
HI, LO = 0, 1
ALPHA = 2.0


def conditional_ffn(nc, x, ids, wi, wo, c_wi_a, c_wi_b, c_wo_a, c_wo_b, e_wi_a, e_wi_b, e_wo_a, e_wo_b, out):
    P = 128
    B, S, D = x.shape
    F = wi.shape[0]
    E, R, _ = e_wi_a.shape
    KD = D // P
    MF = F // P
    PAIR = 2
    T = PAIR * S
    TT = T // P
    STEPS = B // PAIR
    ER = E * R
    LOW = 4 * R
    KL = 3 * R
    WIN = D + R
    WC = R + D + R
    BANK = 512
    PB = BANK // P
    assert ER == P and T == BANK and STEPS * PAIR == B and 2 * LOW == P and 2 * R == 32

    B_PART, B_LO, LOW_LO = [HI, HI, LO, HI], 2 * R, 0
    BO_PART, BO_LO, TL_LO = [LO, HI, HI], 0, 2 * R
    WIN_AT = [0, R]
    OUT_AT = [R, 0]
    RANK_AT = [0, D]

    xv = x.rearrange("b s d -> (b s) d").rearrange("(q t p) d -> q p t d", p=P, t=TT)
    ov = out.rearrange("b s d -> (b s) d").rearrange("(q t p) d -> q t p d", p=P, t=TT)

    bi_parts = nc.dram_tensor("bi_parts", [2, ER, F], F32, kind="Internal").ap()
    bo_parts = nc.dram_tensor("bo_parts", [2, ER, D], F32, kind="Internal").ap()

    with ExitStack() as ctx:
        def sb(name, shape, dt=F32):
            return ctx.enter_context(nc.sbuf_tensor(name, shape, dt))

        def sem(name):
            return ctx.enter_context(nc.semaphore(name))

        bank_h = [ctx.enter_context(nc.psum_tensor(f"bank_h{i}", [P, BANK], F32)) for i in range(4)]
        bank_o = [ctx.enter_context(nc.psum_tensor(f"bank_o{i}", [P, BANK], F32)) for i in range(2)]
        bank_x = [ctx.enter_context(nc.psum_tensor(f"bank_x{i}", [P, BANK], F32)) for i in range(2)]
        out_bank = [bank_h[0], bank_h[1], bank_o[0], bank_o[1]]
        tl_bank = [bank_h[2], bank_h[3], bank_h[2], bank_h[3]]

        ident = sb("ident", [P, P])
        idt = sb("idt", [1, B], I32)
        wi_nat = sb("wi_nat", [P, MF, D])
        wo_nat = sb("wo_nat", [P, KD, F])
        ai_nat = sb("ai_nat", [ER, D])
        aic_nat = sb("aic_nat", [R, D])
        ao_nat = sb("ao_nat", [ER, F])
        aoc_nat = sb("aoc_nat", [KL, F])
        bi_raw = sb("bi_raw", [P, E, MF * R])
        bi_nat = sb("bi_nat", [P, MF, ER])
        bic_nat = sb("bic_nat", [P, MF, R])
        bo_raw = sb("bo_raw", [P, E, KD * R])
        bo_nat = sb("bo_nat", [P, KD, ER])
        boc_nat = sb("boc_nat", [P, KD, R])
        bi0_raw = sb("bi0_raw", [P, PAIR, MF, R])
        bi0_nat = sb("bi0_nat", [P, PAIR, MF, P])
        bo0_raw = sb("bo0_raw", [P, PAIR, KD, R])
        bo0_nat = sb("bo0_nat", [P, PAIR, KD, KL])
        boc0_nat = sb("boc0_nat", [P, KD, KL])
        wiT = [sb(f"wiT{s}", [P, KD, F], F32R) for s in (HI, LO)]
        aiT = [sb(f"aiT{s}", [P, KD * ER + KD * R], F32R) for s in (HI, LO)]
        aoT = [sb(f"aoT{s}", [P, MF, ER], F32R) for s in (HI, LO)]
        biT = [sb(f"biT{s}", [ER, F], F32R) for s in (HI, LO)]
        boT = [sb(f"boT{s}", [ER, D], F32R) for s in (HI, LO)]
        aoc_stack = sb("aoc_stack", [KL, F], F32R)
        boc_stack = sb("boc_stack", [KL, D], F32R)
        wcat = [sb(f"wcat{s}", [P, MF, WC], F32R) for s in (HI, LO)]
        ai_stack = sb("ai_stack", [P, PAIR, KD, P], F32R)
        bi_stack = sb("bi_stack", [P, PAIR, F], F32R)
        bo_stack = sb("bo_stack", [KL, PAIR, D], F32R)
        x_nat = sb("x_nat", [P, TT, D])
        x_res = sb("x_res", [P, TT, D])
        xT = [sb(f"xT{s}", [P, KD, T], F32R) for s in (HI, LO)]
        low_stack = sb("low_stack", [P, T], F32R)
        hid = [sb(f"hid{s}", [P, MF, T], F32R) for s in (HI, LO)]
        lo_sb = sb("lo_sb", [P, P // R, R])
        lo_stack = [sb(f"lo_stack{i}", [KL, P], F32R) for i in range(2)]
        o_sb = sb("o_sb", [P, TT, D])

        ids_in, x_in = sem("ids_in"), sem("x_in")
        wi_in = [sem(f"wi_in{i}") for i in range(2)]
        wo_in, ai_in, ao_in, bi_in, bo_in = (sem(n) for n in ("wo_in", "ai_in", "ao_in", "bi_in", "bo_in"))
        bi0_in, bo0_in, bic_in, boc_in, aoc_in = (sem(n) for n in ("bi0_in", "bo0_in", "bic_in", "boc_in", "aoc_in"))
        ident_zero, ident_ready = sem("ident_zero"), sem("ident_ready")
        nat_ready = sem("nat_ready")
        wt_done, wt_hi, wt_out = sem("wt_done"), sem("wt_hi"), sem("wt_out")
        aoc_hi, aoc_lo = sem("aoc_hi"), sem("aoc_lo")
        common_ready = sem("common_ready")
        parts_out = sem("parts_out")
        ai_ready, ao_ready = sem("ai_ready"), [sem(f"ao_ready{b}") for b in range(PAIR)]
        bi_loaded, bo_loaded = sem("bi_loaded"), [sem(f"bo_loaded{b}") for b in range(PAIR)]
        res_ready = sem("res_ready")
        xt_done, xt_hi, xt_lo = sem("xt_done"), sem("xt_hi"), sem("xt_lo")
        low_done, low_hi, low_lo = sem("low_done"), sem("low_hi"), sem("low_lo")
        up_done, hid_hi, hid_lo = sem("up_done"), sem("hid_hi"), sem("hid_lo")
        main_done, lo_copied = sem("main_done"), sem("lo_copied")
        tl_done, tl_hi, tl_lo = sem("tl_done"), sem("tl_hi"), sem("tl_lo")
        fin_done, added, stored = sem("fin_done"), sem("added"), sem("stored")

        def group(name, bank, wait, tiles=(), products=(), hi=(), lo=(), add=()):
            return dict(name=name, bank=bank, wait=wait, tiles=tiles, products=products, hi=hi, lo=lo, add=add)

        def scatter(ap, n, at=0):
            def view(t):
                return t.rearrange("n (p j) -> n j p", j=n)[:, at:at + PB, :]
            return view(ap)

        def g_wi(k, half, bank):
            tiles = [(bank[:, i * P:(i + 1) * P], wi_nat[:, half * PB + i, k * P:(k + 1) * P]) for i in range(PB)]
            to = [wiT[s][:, k, half * BANK:(half + 1) * BANK] for s in (HI, LO)]
            return group(f"wi{k}{half}", bank, [(wi_in[half], 16)], tiles, hi=[(to[HI], bank[:, :], None)],
                         lo=[(to[LO], bank[:, :], to[HI], None)])

        def g_ai(bank):
            n = KD * ER + KD * R
            tiles = [(bank[:, k * ER:(k + 1) * ER], ai_nat[:, k * P:(k + 1) * P]) for k in range(KD)]
            tiles += [(bank[:, KD * ER + k * R:KD * ER + (k + 1) * R], aic_nat[:, k * P:(k + 1) * P]) for k in range(KD)]
            return group("ai", bank, [(ai_in, 32)], tiles, hi=[(aiT[HI][:, :], bank[:, 0:n], None)],
                         lo=[(aiT[LO][:, :], bank[:, 0:n], aiT[HI][:, :], None)])

        def g_bi0(b, half, bank):
            tiles = [(bank[:, i * P:(i + 1) * P], bi0_nat[:, b, half * PB + i, :]) for i in range(PB)]
            def rows(ap, at, n):
                return scatter(ap[at:at + n, b, :], MF, half * PB)
            src = bank[:, :].rearrange("n (j p) -> n j p", p=P)
            return group(f"bi0{b}{half}", bank, [(nat_ready, b + 1)], tiles, hi=[(rows(bi_stack, 0, P), src, None)],
                         lo=[(rows(bi_stack, at, R), src[at:at + R], rows(bi_stack, at, R), None)
                             for at in (B_LO, LOW + B_LO)])

        def columns_pk(ap):
            return ap.rearrange("n (p k) -> n k p", k=KD)

        def g_bo0(bank):
            tiles = [(bank[0:KL, (b * KD + k) * P:(b * KD + k + 1) * P], bo0_nat[:, b, k, :])
                     for b in range(PAIR) for k in range(KD)]
            hi, lo = [], []
            for b in range(PAIR):
                src = bank[0:KL, b * KD * P:(b + 1) * KD * P].rearrange("n (k p) -> n k p", p=P)
                lo_rows = columns_pk(bo_stack[BO_LO:BO_LO + R, b, :])
                hi.append((columns_pk(bo_stack[:, b, :]), src, None))
                lo.append((lo_rows, src[BO_LO:BO_LO + R], lo_rows, None))
            return group("bo0", bank, [(nat_ready, 3)], tiles, hi=hi, lo=lo)

        def g_boc(bank):
            tiles = [(bank[0:KL, k * P:(k + 1) * P], boc0_nat[:, k, :]) for k in range(KD)]
            src = bank[0:KL, 0:KD * P].rearrange("n (k p) -> n k p", p=P)
            lo_rows = columns_pk(boc_stack[BO_LO:BO_LO + R, :])
            return group("boc", bank, [(nat_ready, 3)], tiles, hi=[(columns_pk(boc_stack[:, :]), src, ALPHA)],
                         lo=[(lo_rows, src[BO_LO:BO_LO + R], lo_rows, ALPHA)])

        def g_fold(k, half, bank):
            f = slice(half * BANK, (half + 1) * BANK)
            wait = [(aoc_lo, 1), (wt_out, OUT["boc"])] if (k, half) == (0, 0) else []
            return group(f"fold{k}{half}", bank, wait,
                         products=[(bank[:, :], boc_stack[:, k * P:(k + 1) * P], aoc_stack[:, f])],
                         add=[(wo_nat[:, k, f], bank[:, :])])

        def g_wo(i, bank):
            tiles = [(bank[:, (jj * KD + k) * P:(jj * KD + k + 1) * P], wo_nat[:, k, (2 * i + jj) * P:(2 * i + jj + 1) * P])
                     for jj in range(2) for k in range(KD)]
            to = [wcat[s][:, 2 * i:2 * i + 2, R:R + D] for s in (HI, LO)]
            src = bank[:, :].rearrange("p (j d) -> p j d", d=D)
            return group(f"wo{i}", bank, [(wt_out, OUT["fold11"])] if i == 0 else [], tiles,
                         hi=[(to[HI], src, None)], lo=[(to[LO], src, to[HI], None)])

        def g_ao(half, bank):
            tiles = [(bank[:, i * ER:(i + 1) * ER], ao_nat[:, (half * PB + i) * P:(half * PB + i + 1) * P]) for i in range(PB)]
            to = [aoT[s][:, half * PB:(half + 1) * PB, :] for s in (HI, LO)]
            src = bank[:, :].rearrange("p (j n) -> p j n", n=ER)
            return group(f"ao{half}", bank, [(ao_in, 16)], tiles, hi=[(to[HI], src, None)],
                         lo=[(to[LO], src, to[HI], None)])

        def g_bi(half, bank):
            tiles = [(bank[:, i * P:(i + 1) * P], bi_nat[:, half * PB + i, :]) for i in range(PB)]
            src = bank[:, :].rearrange("n (j p) -> n j p", p=P)
            to = [scatter(biT[s][:, :], MF, half * PB) for s in (HI, LO)]
            return group(f"bi{half}", bank, [(nat_ready, 4)], tiles, hi=[(to[HI], src, None)],
                         lo=[(to[LO], src, to[HI], None)])

        def g_bo(bank):
            tiles = [(bank[:, k * P:(k + 1) * P], bo_nat[:, k, :]) for k in range(KD)]
            src = bank[:, 0:KD * P].rearrange("n (k p) -> n k p", p=P)
            to = [columns_pk(boT[s][:, :]) for s in (HI, LO)]
            return group("bo", bank, [(nat_ready, 5)], tiles, hi=[(to[HI], src, None)],
                         lo=[(to[LO], src, to[HI], None)])

        ORDER = ["wi00", "wi10", "wi01", "wi11", "ai", "bi000", "bi001", "bi010", "bi011", "bo0", "boc",
                 "fold00", "fold01", "fold10", "fold11", "ao0", "ao1", "wo0", "wo1", "wo2", "wo3", "bo", "bi0", "bi1"]
        OUT = {name: n + 1 for n, name in enumerate(ORDER)}
        HIS = {name: n + 1 for n, name in enumerate(x for x in ORDER if not x.startswith("fold"))}
        o0, o1, x0, x1 = bank_o[0], bank_o[1], bank_x[0], bank_x[1]
        G = {g["name"]: g for g in (
            g_wi(0, 0, bank_h[0]), g_wi(1, 0, bank_h[1]), g_wi(0, 1, bank_h[2]), g_wi(1, 1, bank_h[3]),
            g_ai(o0), g_bi0(0, 0, o1), g_bi0(0, 1, x1), g_bi0(1, 0, o0), g_bi0(1, 1, o1), g_bo0(x1), g_boc(o0),
            g_fold(0, 0, o1), g_fold(0, 1, x1), g_fold(1, 0, x0), g_fold(1, 1, o0), g_ao(0, o1), g_ao(1, x1),
            g_wo(0, x0), g_wo(1, o0), g_wo(2, o1), g_wo(3, x1), g_bo(x0), g_bi(0, o0), g_bi(1, o1))}
        before, last_in = {}, {}
        for name in ORDER:
            key = G[name]["bank"].name
            before[name] = last_in.get(key)
            last_in[key] = name
        FIRST = ["wi00", "wi10", "wi01", "wi11", "ai", ("main", 0), "bi000", "bi001", ("main", 1), ("low",),
                 "bi010", "bi011", ("main", 2), "bo0", "boc", ("main", 3), ("lora", 0), ("lora", 1),
                 "fold00", "fold01", ("main", 4), ("lora", 2), ("lora", 3), "fold10", "fold11",
                 ("main", 5), ("lora", 4), "ao0", "ao1", ("main", 6), ("lora", 5), "wo0", "wo1",
                 ("main", 7), ("lora", 6), "wo2", "wo3", ("lora", 7), "bo", "bi0", "bi1"]

        block = ctx.enter_context(nc.Block())

        @block.sync
        def _(sp):
            sp.dma_start(idt[:, :], ids.rearrange("(o n) -> o n", o=1)).then_inc(ids_in, 16)
            sp.dma_start(wi_nat[:, 0:MF // 2, :], wi.rearrange("(j p) d -> p j d", p=P)[:, 0:MF // 2, :]).then_inc(wi_in[0], 16)
            sp.wait_ge(ids_in, 16)
            first = [sp.value_load(idt[0:1, b:b + 1], min_val=0, max_val=E - 1) for b in range(PAIR)]
            for b in range(PAIR):
                sp.dma_start(bi0_raw[:, b, :, :], e_wi_b[bass.ds(first[b], 1), :, :].rearrange("o (p j) r -> (o p) j r", p=P)
                             ).then_inc(bi0_in, 16)
            sp.dma_start(bic_nat[:, :, :], c_wi_b.rearrange("(p j) r -> p j r", p=P)).then_inc(bic_in, 16)
            for b in range(PAIR):
                sp.dma_start(bo0_raw[:, b, :, :], e_wo_b[bass.ds(first[b], 1), :, :].rearrange("o (p k) r -> (o p) k r", p=P)
                             ).then_inc(bo0_in, 16)
            sp.dma_start(wo_nat[:, :, :], wo.rearrange("(k p) f -> p k f", p=P)).then_inc(wo_in, 16)
            sp.dma_start(bi_raw[:, :, :], e_wi_b.rearrange("e (p j) r -> p e (j r)", p=P)).then_inc(bi_in, 16)
            sp.dma_start(bo_raw[:, :, :], e_wo_b.rearrange("e (p k) r -> p e (k r)", p=P)).then_inc(bo_in, 16)

            def expert_rows(step):
                rows = []
                for b in range(PAIR):
                    e = sp.value_load(idt[0:1, bass.ds(step * PAIR + b, 1)], min_val=0, max_val=E - 1)
                    rows.append(sp.snap(e * R))
                return rows

            def load_bi(rows):
                for b in range(PAIR):
                    for i, s in enumerate(B_PART):
                        sp.dma_start(bi_stack[i * R:(i + 1) * R, b, :].bitcast(F32),
                                     bi_parts[s, bass.ds(rows[b], R), :]).then_inc(bi_loaded, 16)

            def load_bo(rows, b):
                for i, s in enumerate(BO_PART):
                    at = i * R
                    sp.dma_start(bo_stack[at:at + R, b, :].bitcast(F32),
                                 bo_parts[s, bass.ds(rows[b], R), :]).then_inc(bo_loaded[b], 16)

            def store(step, t):
                sp.wait_ge(added, step * TT + t + 1)
                sp.dma_start(ov[step, t] if isinstance(step, int) else ov[bass.ds(step, 1), t, :, :].rearrange("o p d -> (o p) d"),
                             o_sb[:, t, :]).then_inc(stored, 16)

            sp.wait_ge(wt_out, OUT["bo"])
            for s in (HI, LO):
                sp.dma_start(bo_parts[s], boT[s][:, :].bitcast(F32)).then_inc(parts_out, 16)
            sp.wait_ge(wt_out, OUT["bi1"])
            for s in (HI, LO):
                sp.dma_start(bi_parts[s], biT[s][:, :].bitcast(F32)).then_inc(parts_out, 16)

            with sp.Fori(0, STEPS - 1) as q:
                rows = expert_rows(q + 1)
                sp.wait_ge(res_ready, q + 1)
                sp.wait_ge(xt_done, (q + 1) * KD)
                sp.dma_start(x_nat[:, :, :], xv[bass.ds(q + 1, 1), :, :, :].rearrange("o p t d -> (o p) t d")).then_inc(x_in, 16)
                sp.wait_ge(up_done, (q + 1) * MF)
                sp.wait_ge(parts_out, 64)
                load_bi(rows)
                store(q, 0)
                store(q, 1)
                sp.wait_ge(fin_done, q * TT + 2)
                load_bo(rows, 0)
                store(q, 2)
                store(q, 3)
                sp.wait_ge(fin_done, q * TT + 4)
                load_bo(rows, 1)
            for t in range(TT):
                store(STEPS - 1, t)
            sp.wait_ge(stored, STEPS * TT * 16)

        @block.gpsimd
        def _(pool):
            nc.gpsimd.memset(ident[:, :], 0.0).then_inc(ident_zero, 1)
            pool.wait_ge(ident_zero, 1)
            nc.gpsimd.affine_select(out=ident[:, :], in_=ident[:, :], compare_op=ALU.not_equal, fill=1.0, base=0,
                                    pattern=[[-1, P]], channel_multiplier=1).then_inc(ident_ready, 1)

            def spread_ai(b, at, src):
                hi, lo = (src(s).bitcast(F32) for s in (HI, LO))
                nc.gpsimd.tensor_copy(
                    ai_stack[:, b, :, at:at + 3 * R].rearrange("p k (i r) -> p k i r", r=R),
                    hi.unsqueeze(2).broadcast_to([P, KD, 3, R]))
                return nc.gpsimd.tensor_copy(ai_stack[:, b, :, at + 3 * R:at + 4 * R], lo)

            def experts(step):
                return [pool.value_load(idt[0:1, bass.ds(step * PAIR + b, 1)], min_val=0, max_val=E - 1)
                        for b in range(PAIR)]

            def copy_ai(at):
                for b in range(PAIR):
                    last = spread_ai(b, 0, lambda s: aiT[s][:, 0:KD * ER].rearrange("p (k n) -> p k n", k=KD)[
                        :, :, bass.ds(at[b], R)])
                last.then_inc(ai_ready, 1)

            def copy_ao(at, b):
                to = [0, R + D][b]
                for s in (HI, LO):
                    last = nc.gpsimd.tensor_copy(wcat[s][:, :, to:to + R], aoT[s][:, :, bass.ds(at[b], R)].bitcast(F32))
                last.then_inc(ao_ready[b], 1)

            def spread(to, src, blocks):
                return nc.gpsimd.tensor_copy(to.rearrange("p j (i r) -> p j i r", r=R),
                                             src.unsqueeze(2).broadcast_to([P, src.shape[1], blocks, R]))

            def spread_bi0(b):
                spread(bi0_nat[:, b, :, 0:LOW], bi0_raw[:, b, :, :], 4)
                spread(bi0_nat[:, b, :, LOW:P], bic_nat[:, :, :], 4).then_inc(nat_ready, 1)

            pool.wait_ge(bi0_in, 32)
            pool.wait_ge(bic_in, 16)
            spread_bi0(0)
            pool.wait_ge(ids_in, 16)
            pool.wait_ge(wt_out, OUT["ai"])
            for b in range(PAIR):
                last = spread_ai(b, LOW, lambda s: aiT[s][:, KD * ER:].rearrange("p (k n) -> p k n", k=KD))
            last.then_inc(common_ready, 1)
            at = [pool.snap(e * R) for e in experts(0)]
            copy_ai(at)
            spread_bi0(1)
            pool.wait_ge(bo0_in, 32)
            pool.wait_ge(boc_in, 16)
            for b in range(PAIR):
                spread(bo0_nat[:, b, :, :], bo0_raw[:, b, :, :], 3)
            spread(boc0_nat[:, :, :], boc_nat[:, :, :], 3).then_inc(nat_ready, 1)
            pool.wait_ge(bi_in, 16)
            nc.gpsimd.tensor_copy(bi_nat[:, :, :].rearrange("p j (e r) -> p j e r", r=R),
                                  bi_raw[:, :, :].rearrange("p e (j r) -> p j e r", r=R)).then_inc(nat_ready, 1)
            pool.wait_ge(bo_in, 16)
            nc.gpsimd.tensor_copy(bo_nat[:, :, :].rearrange("p k (e r) -> p k e r", r=R),
                                  bo_raw[:, :, :].rearrange("p e (k r) -> p k e r", r=R)).then_inc(nat_ready, 1)
            pool.wait_ge(wt_out, OUT["ao1"])
            for b in range(PAIR):
                copy_ao(at, b)
            with pool.Fori(0, STEPS - 1) as q:
                at = [pool.snap(e * R) for e in experts(q + 1)]
                pool.wait_ge(low_done, q + 1)
                copy_ai(at)
                pool.wait_ge(main_done, q * TT + 2)
                copy_ao(at, 0)
                pool.wait_ge(main_done, q * TT + 4)
                copy_ao(at, 1)

        @block.scalar
        def _(act):
            act.dma_start(x_nat[:, :, :], xv[0]).then_inc(x_in, 16)
            act.dma_start(wi_nat[:, MF // 2:, :], wi.rearrange("(j p) d -> p j d", p=P)[:, MF // 2:, :]).then_inc(wi_in[1], 16)
            act.dma_start(ai_nat[:, :], e_wi_a.rearrange("e r d -> (e r) d")).then_inc(ai_in, 16)
            act.dma_start(aic_nat[:, :], c_wi_a).then_inc(ai_in, 16)
            act.dma_start(boc_nat[:, :, :], c_wo_b.rearrange("(p k) r -> p k r", p=P)).then_inc(boc_in, 16)
            for i in range(3):
                act.dma_start(aoc_nat[i * R:(i + 1) * R, :], c_wo_a).then_inc(aoc_in, 16)
            act.dma_start(ao_nat[:, :], e_wo_a.rearrange("e r f -> (e r) f")).then_inc(ao_in, 16)

            def group_hi(name):
                g = G[name]
                if g["hi"]:
                    act.wait_ge(wt_done, OUT[name])
                    for out_, src, scale in g["hi"]:
                        last = nc.scalar.copy(out_, src) if scale is None else nc.scalar.mul(out_, src, scale)
                    last.then_inc(wt_hi, 1)

            def x_hi(step):
                for k in range(KD):
                    act.wait_ge(xt_done, step * KD + k + 1)
                    nc.scalar.copy(xT[HI][:, k, :], bank_x[k][:, :]).then_inc(xt_hi, 1)

            def lowi_hi(step):
                act.wait_ge(low_done, step + 1)
                nc.scalar.mul(low_stack[:, :], bank_x[0][:, :], ALPHA).then_inc(low_hi, 1)

            def hidden_hi(step, m):
                act.wait_ge(up_done, step * MF + m + 1)
                nc.scalar.activation(hid[HI][:, m, :], bank_h[m % 4][:, :], ACT.Relu).then_inc(hid_hi, 1)

            def low_copy(step, t):
                act.wait_ge(main_done, step * TT + t + 1)
                at = RANK_AT[t // (TT // PAIR)]
                ranks = out_bank[t][:, at:at + R]
                nc.scalar.copy(lo_sb[:, :, :], ranks.unsqueeze(1).broadcast_to([P, P // R, R])).then_inc(lo_copied, 1)

            def tl_part(step, t):
                act.wait_ge(tl_done, step * TT + t + 1)
                nc.scalar.mul(lo_stack[t % 2][:, :], tl_bank[t][0:KL, 0:P], ALPHA).then_inc(tl_hi, 1)

            def down(step, more):
                low_copy(step, 0)
                tl_part(step, 0)
                if more:
                    x_hi(step + 1)
                for t in range(1, TT):
                    low_copy(step, t)
                    tl_part(step, t)
                if more:
                    lowi_hi(step + 1)

            x_hi(0)
            for what in FIRST:
                if isinstance(what, str):
                    group_hi(what)
                    if what == "boc":
                        act.wait_ge(aoc_in, 3 * 16)
                        nc.scalar.copy(aoc_stack[:, :], aoc_nat[:, :]).then_inc(aoc_hi, 1)
                elif what[0] == "low":
                    lowi_hi(0)
                elif what[0] == "lora":
                    hidden_hi(0, what[1])
            with act.Fori(0, STEPS - 1) as q:
                down(q, True)
                for m in range(MF):
                    hidden_hi(q + 1, m)
            down(STEPS - 1, False)

        @block.vector
        def _(dve):
            def lo_part(out_, src, scale, hi):
                op = ALU.max if scale is None else ALU.mult
                return nc.vector.scalar_tensor_tensor(out=out_, in0=src, scalar=0.0 if scale is None else scale,
                                                      in1=hi.bitcast(F32), op0=op, op1=ALU.subtract)

            def group_out(name):
                g = G[name]
                if g["add"]:
                    dve.wait_ge(wt_done, OUT[name])
                    dve.wait_ge(wo_in, 16)
                    for part, src in g["add"]:
                        last = nc.vector.tensor_tensor(part, src, part, ALU.add)
                else:
                    dve.wait_ge(wt_hi, HIS[name])
                    for out_, src, hi, scale in g["lo"]:
                        last = (nc.vector.tensor_tensor(out_, src, hi.bitcast(F32), ALU.subtract) if scale is None
                                else lo_part(out_, src, scale, hi))
                last.then_inc(wt_out, 1)

            def x_lo(step):
                for k in range(KD):
                    dve.wait_ge(xt_hi, step * KD + k + 1)
                    nc.vector.tensor_tensor(xT[LO][:, k, :], bank_x[k][:, :], xT[HI][:, k, :].bitcast(F32),
                                            ALU.subtract).then_inc(xt_lo, 1)

            def keep_x(step):
                dve.wait_ge(x_in, (step + 1) * 16)
                if not isinstance(step, int):
                    dve.wait_ge(added, step * TT)
                nc.vector.tensor_copy(x_res[:, :, :], x_nat[:, :, :]).then_inc(res_ready, 1)

            def lowi_lo(step):
                dve.wait_ge(low_hi, step + 1)
                for at in (LOW_LO, LOW + LOW_LO):
                    rows = low_stack[at:at + R, :]
                    lo_part(rows, bank_x[0][at:at + R, :], ALPHA, rows).then_inc(low_lo, 1)

            def hidden_lo(step, m):
                dve.wait_ge(hid_hi, step * MF + m + 1)
                lo_part(hid[LO][:, m, :], bank_h[m % 4][:, :], None, hid[HI][:, m, :]).then_inc(hid_lo, 1)

            def tl_lo_part(step, t):
                dve.wait_ge(tl_hi, step * TT + t + 1)
                rows = lo_stack[t % 2][TL_LO:KL, :]
                lo_part(rows, tl_bank[t][TL_LO:KL, 0:P], ALPHA, rows).then_inc(tl_lo, 1)

            def add(step, t):
                b = t // (TT // PAIR)
                dve.wait_ge(fin_done, step * TT + t + 1)
                if t == 0:
                    dve.wait_ge(res_ready, step + 1)
                    dve.wait_ge(stored, step * TT * 16)
                nc.vector.tensor_tensor(o_sb[:, t, :], out_bank[t][:, OUT_AT[b]:OUT_AT[b] + D], x_res[:, t, :],
                                        ALU.add).then_inc(added, 1)

            def down(step, more):
                tl_lo_part(step, 0)
                if more:
                    x_lo(step + 1)
                add(step, 0)
                tl_lo_part(step, 1)
                add(step, 1)
                tl_lo_part(step, 2)
                tl_lo_part(step, 3)
                add(step, 2)
                add(step, 3)
                if more:
                    lowi_lo(step + 1)
                    keep_x(step + 1)

            x_lo(0)
            for what in FIRST:
                if isinstance(what, str):
                    group_out(what)
                    if what == "boc":
                        dve.wait_ge(aoc_hi, 1)
                        rows = aoc_stack[TL_LO:KL, :]
                        nc.vector.tensor_tensor(rows, aoc_nat[TL_LO:KL, :], rows.bitcast(F32), ALU.subtract).then_inc(aoc_lo, 1)
                elif what[0] == "low":
                    lowi_lo(0)
                    keep_x(0)
                elif what[0] == "lora":
                    hidden_lo(0, what[1])
            with dve.Fori(0, STEPS - 1) as q:
                down(q, True)
                for m in range(MF):
                    hidden_lo(q + 1, m)
            down(STEPS - 1, False)

        @block.tensor
        def _(pe):
            def run_group(name):
                g = G[name]
                for s, v in g["wait"]:
                    pe.wait_ge(s, v)
                if before[name]:
                    pe.wait_ge(wt_out, OUT[before[name]])
                for dst, src in g["tiles"]:
                    last = nc.tensor.transpose(dst, src, ident[0:src.shape[0], 0:src.shape[0]])
                for dst, lhsT, rhs in g["products"]:
                    last = nc.tensor.matmul(dst, lhsT, rhs, start=True, stop=True)
                last.then_inc(wt_done, 1)

            def transpose_x(step):
                pe.wait_ge(x_in, (step + 1) * 16)
                for k in range(KD):
                    for t in range(TT):
                        last = nc.tensor.transpose(bank_x[k][:, t * P:(t + 1) * P], x_nat[:, t, k * P:(k + 1) * P],
                                                   ident[:, :])
                    last.then_inc(xt_done, 1)

            def low_in(step, b):
                if b == 0:
                    pe.wait_ge(xt_lo, (step + 1) * KD)
                    pe.wait_ge(ai_ready, step + 1)
                cols = slice(b * S, (b + 1) * S)
                for k in range(KD):
                    for s in (HI, LO):
                        last = nc.tensor.matmul(bank_x[0][:, cols], ai_stack[:, b, k, :], xT[s][:, k, cols],
                                                start=(k == 0 and s == HI), stop=(k == KD - 1 and s == LO))
                if b == PAIR - 1:
                    last.then_inc(low_done, 1)

            def up_main(step, m):
                if m >= 4:
                    pe.wait_ge(hid_lo, step * MF + m - 3)
                f = slice(m * P, (m + 1) * P)
                for i, (k, sw, sx) in enumerate((k, sw, sx) for k in range(KD)
                                                for sw, sx in ((HI, HI), (HI, LO), (LO, HI))):
                    nc.tensor.matmul(bank_h[m % 4][:, :], wiT[sw][:, k, f], xT[sx][:, k, :], start=(i == 0), stop=False)

            def up_lora(step, m):
                if m == 0:
                    pe.wait_ge(low_lo, (step + 1) * 2)
                    if isinstance(step, int):
                        pe.wait_ge(wt_out, OUT["bi011"])
                    else:
                        pe.wait_ge(bi_loaded, step * PAIR * 4 * 16)
                for b in range(PAIR):
                    cols = slice(b * S, (b + 1) * S)
                    last = nc.tensor.matmul(bank_h[m % 4][:, cols], bi_stack[:, b, m * P:(m + 1) * P],
                                            low_stack[:, cols], start=False, stop=(b == PAIR - 1))
                last.then_inc(up_done, 1)

            def up(step):
                for m in range(MF + 1):
                    if m < MF:
                        up_main(step, m)
                    if m > 0:
                        up_lora(step, m - 1)

            def first_up():
                for what in FIRST:
                    if isinstance(what, str):
                        if what == "bi001":
                            pe.wait_ge(xt_lo, KD)
                        if what == "fold10":
                            pe.wait_ge(low_lo, 2)
                        run_group(what)
                    elif what[0] == "low":
                        pe.wait_ge(common_ready, 1)
                        low_in(0, 0)
                        low_in(0, 1)
                    elif what[0] == "lora":
                        up_lora(0, what[1])
                    else:
                        m = what[1]
                        if m == 0:
                            pe.wait_ge(xt_lo, KD)
                            pe.wait_ge(wt_out, OUT["wi10"])
                        if m == 2:
                            pe.wait_ge(wt_out, OUT["wi11"])
                        up_main(0, m)

            def main(step, t):
                b = t // (TT // PAIR)
                tok = slice(t * P, (t + 1) * P)
                win = slice(WIN_AT[b], WIN_AT[b] + WIN)
                if t % (TT // PAIR) == 0:
                    pe.wait_ge(ao_ready[b], step + 1)
                if t == 1:
                    pe.wait_ge(hid_lo, step * MF + 6)
                if t == 2:
                    pe.wait_ge(wt_out, OUT["bi1"])
                    pe.wait_ge(added, step * TT)
                for m in range(MF):
                    if t == 0:
                        pe.wait_ge(hid_lo, step * MF + max(m + 1, 5))
                    for i, (sh, sw) in enumerate(((HI, HI), (HI, LO), (LO, HI))):
                        last = nc.tensor.matmul(out_bank[t][:, 0:WIN], hid[sh][:, m, tok], wcat[sw][:, m, win],
                                                start=(m == 0 and i == 0), stop=(m == MF - 1 and i == 2))
                last.then_inc(main_done, 1)

            def turn_low(step, t):
                pe.wait_ge(lo_copied, step * TT + t + 1)
                if t < 2:
                    pe.wait_ge(hid_lo, step * MF + 7 + t)
                nc.tensor.transpose(tl_bank[t][:, 0:P], lo_sb[:, :, :].rearrange("p i r -> p (i r)"),
                                    ident[:, :]).then_inc(tl_done, 1)

            def fin(step, t):
                b = t // (TT // PAIR)
                pe.wait_ge(tl_lo, step * TT + t + 1)
                if t % (TT // PAIR) == 0:
                    pe.wait_ge(bo_loaded[b], step * 3 * 16)
                nc.tensor.matmul(out_bank[t][:, OUT_AT[b]:OUT_AT[b] + D], lo_stack[t % 2][:, :], bo_stack[:, b, :],
                                 start=False, stop=True, skip_group_check=True).then_inc(fin_done, 1)

            def down(step, more):
                main(step, 0)
                main(step, 1)
                turn_low(step, 0)
                if more:
                    transpose_x(step + 1)
                main(step, 2)
                fin(step, 0)
                turn_low(step, 1)
                main(step, 3)
                fin(step, 1)
                turn_low(step, 2)
                if more:
                    low_in(step + 1, 0)
                turn_low(step, 3)
                fin(step, 2)
                if more:
                    low_in(step + 1, 1)
                fin(step, 3)

            pe.wait_ge(ident_ready, 1)
            transpose_x(0)
            first_up()
            pe.wait_ge(wt_out, OUT["wo3"])
            with pe.Fori(0, STEPS - 1) as q:
                down(q, True)
                up(q + 1)
            down(STEPS - 1, False)


_INS = ["x", "itok_B_0_7", "L0_cond_wi", "L0_cond_wo", "L0_cond_common_wi_a", "L0_cond_common_wi_b",
        "L0_cond_common_wo_a", "L0_cond_common_wo_b", "L0_cond_experts_wi_a", "L0_cond_experts_wi_b",
        "L0_cond_experts_wo_a", "L0_cond_experts_wo_b"]


def kernel(**inputs):
    import numpy as np
    import concourse.bacc as bacc
    from concourse.bass_utils import run_bass_kernel_spmd

    nc = bacc.Bacc("TRN2", target_bir_lowering=False, num_devices=1)
    arrays, args = {}, []
    for name in _INS:
        a = np.ascontiguousarray(inputs[name])
        arrays[f"in_{name}"] = a
        args.append(nc.dram_tensor(f"in_{name}", a.shape, mybir.dt.from_np(a.dtype), kind="ExternalInput").ap())
    args.append(nc.dram_tensor("out_0", inputs["x"].shape, F32, kind="ExternalOutput").ap())
    conditional_ffn(nc, *args)
    result = run_bass_kernel_spmd(nc, [arrays], core_ids=[0])
    return result.results[0]["out_0"]
```

```python
from contextlib import ExitStack

import concourse.bass as bass
from concourse import mybir

F32 = mybir.dt.float32
F32R = mybir.dt.float32r
I32 = mybir.dt.int32
ALU = mybir.AluOpType
ACT = mybir.ActivationFunctionType
HI, LO = 0, 1
ALPHA = 2.0


def conditional_ffn(nc, x, ids, wi, wo, c_wi_a, c_wi_b, c_wo_a, c_wo_b, e_wi_a, e_wi_b, e_wo_a, e_wo_b, out):
    P = 128
    B, S, D = x.shape
    F = wi.shape[0]
    E, R, _ = e_wi_a.shape
    KD = D // P
    MF = F // P
    PAIR = 2
    T = PAIR * S
    TT = T // P
    SEQ_TILES = TT // PAIR
    STEPS = B // PAIR
    ER = E * R
    BLK = 2 * R
    KL = 3 * R
    WIN = D + R
    WC = R + D + R
    BANK = 512
    FIRST_HALF, SECOND_HALF = range(MF // 2), range(MF // 2, MF)
    WARM_UP = 5
    PB = BANK // P
    WI_LOAD = [0, 1, 2, 2]
    assert ER == P and T == BANK and STEPS * PAIR == B and 4 * BLK == P and 2 * R == 32

    B_PART, B_LO, LOW_LO = [HI, LO, HI, HI], BLK, 2 * BLK
    BO_PART, BO_LO, TL_LO = [LO, HI, HI], 0, 2 * R
    WIN_AT = [0, R]
    OUT_AT = [R, 0]
    RANK_AT = [0, D]

    xv = x.rearrange("(q b) (p u) d -> q b p (u d)", b=PAIR, p=P)
    ov = out.rearrange("(q b) (p u) d -> q b u p d", b=PAIR, p=P)

    bi_parts = nc.dram_tensor("bi_parts", [2, ER, F], F32, kind="Internal").ap()
    bo_parts = nc.dram_tensor("bo_parts", [2, ER, D], F32, kind="Internal").ap()

    with ExitStack() as ctx:
        def sb(name, shape, dt=F32):
            return ctx.enter_context(nc.sbuf_tensor(name, shape, dt))

        def sem(name):
            return ctx.enter_context(nc.semaphore(name))

        bank_h = [ctx.enter_context(nc.psum_tensor(f"bank_h{i}", [P, BANK], F32)) for i in range(4)]
        bank_o = [ctx.enter_context(nc.psum_tensor(f"bank_o{i}", [P, BANK], F32)) for i in range(2)]
        bank_x = [ctx.enter_context(nc.psum_tensor(f"bank_x{i}", [P, BANK], F32)) for i in range(2)]
        out_bank = [bank_h[0], bank_h[1], bank_o[0], bank_o[1]]
        tl_bank = [bank_h[2], bank_h[3], bank_h[2], bank_h[3]]

        ident = sb("ident", [P, P])
        zeros = sb("zeros", [P, P])
        act_warm = sb("act_warm", [P, 1])
        idt = sb("idt", [1, B], I32)
        wi_nat = sb("wi_nat", [P, MF, D])
        wo_nat = sb("wo_nat", [P, KD, F])
        ai_nat = sb("ai_nat", [ER, D])
        aic_nat = sb("aic_nat", [R, D])
        ao_nat = sb("ao_nat", [ER, F])
        aoc_nat = sb("aoc_nat", [KL, F])
        bi_raw = sb("bi_raw", [P, E, MF * R])
        bi_nat = sb("bi_nat", [P, MF, ER])
        bic_nat = sb("bic_nat", [P, MF, R])
        bo_raw = sb("bo_raw", [P, E, KD * R])
        bo_nat = sb("bo_nat", [P, KD, ER])
        boc_nat = sb("boc_nat", [P, KD, R])
        bi0_raw = sb("bi0_raw", [P, PAIR, MF, R])
        bi0_nat = sb("bi0_nat", [P, PAIR, MF, P])
        boc0_nat = sb("boc0_nat", [P, KD, KL])
        wiT = [sb(f"wiT{s}", [P, KD, F], F32R) for s in (HI, LO)]
        aiT = [sb(f"aiT{s}", [P, KD * ER + KD * R], F32R) for s in (HI, LO)]
        aoT = [sb(f"aoT{s}", [P, MF, ER], F32R) for s in (HI, LO)]
        biT = [sb(f"biT{s}", [ER, F], F32R) for s in (HI, LO)]
        boT = [sb(f"boT{s}", [ER, D], F32R) for s in (HI, LO)]
        aoc_stack = sb("aoc_stack", [KL, F], F32R)
        boc_stack = sb("boc_stack", [KL, D], F32R)
        wcat = [sb(f"wcat{s}", [P, MF, WC], F32R) for s in (HI, LO)]
        ai_stack = sb("ai_stack", [P, PAIR, KD, P], F32R)
        bi_stack = sb("bi_stack", [P, PAIR, F], F32R)
        bo_stack = sb("bo_stack", [KL, PAIR, D], F32R)
        x_nat = sb("x_nat", [P, TT, D])
        x_res = sb("x_res", [P, TT, D])
        xT = [sb(f"xT{s}", [P, KD, T], F32R) for s in (HI, LO)]
        low_stack = sb("low_stack", [P, T], F32R)
        hid = [sb(f"hid{s}", [P, MF, T], F32R) for s in (HI, LO)]
        lo_sb = [sb(f"lo_sb{i}", [P, P // R, R]) for i in range(2)]
        lo_stack = [sb(f"lo_stack{i}", [KL, P], F32R) for i in range(2)]
        o_sb = sb("o_sb", [P, TT, D])

        ids_in, x_in = sem("ids_in"), [sem(f"x_in{b}") for b in range(PAIR)]
        wi_in = [sem(f"wi_in{i}") for i in range(3)]
        wo_in, ai_in, ao_in, bi_in, bo_in = (sem(n) for n in ("wo_in", "ai_in", "ao_in", "bi_in", "bo_in"))
        bi0_in = [sem(f"bi0_in{b}") for b in range(PAIR)]
        bic_in, boc_in, aoc_in = (sem(n) for n in ("bic_in", "boc_in", "aoc_in"))
        ident_zero, ident_ready = sem("ident_zero"), sem("ident_ready")
        nat_ready, bi0_common = sem("nat_ready"), sem("bi0_common")
        bi0_expert = sem("bi0_expert")
        zeros_ready = sem("zeros_ready")
        wt_done, wt_hi, wt_out = sem("wt_done"), sem("wt_hi"), sem("wt_out")
        aoc_hi, aoc_lo = sem("aoc_hi"), sem("aoc_lo")
        common_ready = sem("common_ready")
        bi_out, bo_out = sem("bi_out"), sem("bo_out")
        ai_ready, ao_ready = sem("ai_ready"), [sem(f"ao_ready{b}") for b in range(PAIR)]
        bi_loaded, bo_loaded = sem("bi_loaded"), [sem(f"bo_loaded{b}") for b in range(PAIR)]
        res_ready = sem("res_ready")
        xt_done, xt_hi, xt_lo = sem("xt_done"), sem("xt_hi"), sem("xt_lo")
        low_done, low_hi, low_lo = sem("low_done"), sem("low_hi"), sem("low_lo")
        up_done, hid_hi, hid_lo = sem("up_done"), sem("hid_hi"), sem("hid_lo")
        main_done, lo_copied = sem("main_done"), sem("lo_copied")
        tl_done, tl_hi, tl_lo = sem("tl_done"), sem("tl_hi"), sem("tl_lo")
        fin_done, added, stored = sem("fin_done"), sem("added"), sem("stored")

        FIRST = ["wi0", ("x",), "ai", ("main", 0), "wi1", ("main", 1), "bi000", "bi001", "bi010", ("low",), "bi011",
                 ("main", 2), "wi2", ("lora", 0), ("main", 3), ("lora", 1), ("lora", 2), "boc", "wi3", "ao0",
                 ("main", 4), ("lora", 3), "wo0", ("main", 5), ("lora", 4), "bo", "wo1", ("main", 6),
                 ("lora", 5), "ao1", "wo2", "wo3", ("main", 7), ("lora", 6), "bi0", ("lora", 7), "bi1"]
        ORDER = [what for what in FIRST if isinstance(what, str)]
        OUT = {name: n + 1 for n, name in enumerate(ORDER)}

        def group(name, bank, wait, tiles=(), products=(), hi=(), lo=()):
            return dict(name=name, bank=bank, wait=wait, tiles=tiles, products=products, hi=hi, lo=lo)

        def scatter(ap, n, at=0):
            def view(t):
                return t.rearrange("n (p j) -> n j p", j=n)[:, at:at + PB, :]
            return view(ap)

        def g_wi(i, bank):
            tiles = [(bank[:, (k * 2 + jj) * P:(k * 2 + jj + 1) * P], wi_nat[:, 2 * i + jj, k * P:(k + 1) * P])
                     for k in range(KD) for jj in range(2)]
            to = [wiT[s][:, :, 2 * i * P:2 * (i + 1) * P] for s in (HI, LO)]
            src = bank[:, :].rearrange("p (k f) -> p k f", k=KD)
            return group(f"wi{i}", bank, [(wi_in[WI_LOAD[i]], 16)], tiles, hi=[(to[HI], src, None)],
                         lo=[(to[LO], src, to[HI], None)])

        def g_ai(bank):
            n = KD * ER + KD * R
            tiles = [(bank[:, k * ER:(k + 1) * ER], ai_nat[:, k * P:(k + 1) * P]) for k in range(KD)]
            tiles += [(bank[:, KD * ER + k * R:KD * ER + (k + 1) * R], aic_nat[:, k * P:(k + 1) * P]) for k in range(KD)]
            return group("ai", bank, [(ai_in, 32)], tiles, hi=[(aiT[HI][:, :], bank[:, 0:n], None)],
                         lo=[(aiT[LO][:, :], bank[:, 0:n], aiT[HI][:, :], None)])

        def g_bi0(b, half, bank):
            tiles = [(bank[:, i * P:(i + 1) * P], bi0_nat[:, b, half * PB + i, :]) for i in range(PB)]
            def rows(ap, at, n):
                return scatter(ap[at:at + n, b, :], MF, half * PB)
            src = bank[:, :].rearrange("n (j p) -> n j p", p=P)
            return group(f"bi0{b}{half}", bank, [(bi0_expert, b + 1), (bi0_common, b + 1)], tiles, hi=[(rows(bi_stack, 0, P), src, None)],
                         lo=[(rows(bi_stack, B_LO, BLK), src[B_LO:B_LO + BLK], rows(bi_stack, B_LO, BLK), None)])

        def columns_pk(ap):
            return ap.rearrange("n (p k) -> n k p", k=KD)

        def g_boc(bank):
            tiles = [(bank[0:KL, k * P:(k + 1) * P], boc0_nat[:, k, :]) for k in range(KD)]
            src = bank[0:KL, 0:KD * P].rearrange("n (k p) -> n k p", p=P)
            lo_rows = columns_pk(boc_stack[BO_LO:BO_LO + R, :])
            return group("boc", bank, [(nat_ready, 1)], tiles, hi=[(columns_pk(boc_stack[:, :]), src, ALPHA)],
                         lo=[(lo_rows, src[BO_LO:BO_LO + R], lo_rows, ALPHA)])

        def g_wo(i, bank):
            tiles = [(bank[:, (jj * KD + k) * P:(jj * KD + k + 1) * P], wo_nat[:, k, (2 * i + jj) * P:(2 * i + jj + 1) * P])
                     for jj in range(2) for k in range(KD)]
            to = [wcat[s][:, 2 * i:2 * i + 2, R:R + D] for s in (HI, LO)]
            src = bank[:, :].rearrange("p (j d) -> p j d", d=D)
            products = [(bank[:, jj * D:(jj + 1) * D], aoc_stack[:, (2 * i + jj) * P:(2 * i + jj + 1) * P], boc_stack[:, :])
                        for jj in range(2)]
            return group(f"wo{i}", bank, [(wo_in, 16), (aoc_lo, 1), (wt_out, OUT["boc"])], tiles, products,
                         hi=[(to[HI], src, None)], lo=[(to[LO], src, to[HI], None)])

        def g_ao(half, bank):
            tiles = [(bank[:, i * ER:(i + 1) * ER], ao_nat[:, (half * PB + i) * P:(half * PB + i + 1) * P]) for i in range(PB)]
            to = [aoT[s][:, half * PB:(half + 1) * PB, :] for s in (HI, LO)]
            src = bank[:, :].rearrange("p (j n) -> p j n", n=ER)
            return group(f"ao{half}", bank, [(ao_in, 16)], tiles, hi=[(to[HI], src, None)],
                         lo=[(to[LO], src, to[HI], None)])

        def g_bi(half, bank):
            tiles = [(bank[:, i * P:(i + 1) * P], bi_nat[:, half * PB + i, :]) for i in range(PB)]
            src = bank[:, :].rearrange("n (j p) -> n j p", p=P)
            to = [scatter(biT[s][:, :], MF, half * PB) for s in (HI, LO)]
            return group(f"bi{half}", bank, [(nat_ready, 3)], tiles, hi=[(to[HI], src, None)],
                         lo=[(to[LO], src, to[HI], None)])

        def g_bo(bank):
            tiles = [(bank[:, k * P:(k + 1) * P], bo_nat[:, k, :]) for k in range(KD)]
            src = bank[:, 0:KD * P].rearrange("n (k p) -> n k p", p=P)
            to = [columns_pk(boT[s][:, :]) for s in (HI, LO)]
            return group("bo", bank, [(nat_ready, 2)], tiles, hi=[(to[HI], src, None)],
                         lo=[(to[LO], src, to[HI], None)])

        o0, o1, x0, x1 = bank_o[0], bank_o[1], bank_x[0], bank_x[1]
        G = {g["name"]: g for g in (
            g_wi(0, o0), g_ai(bank_h[3]), g_wi(1, o1), g_bi0(0, 0, x1), g_bi0(0, 1, o0), g_bi0(1, 0, o1), g_bi0(1, 1, x1),
            g_wi(2, o0), g_boc(o1), g_wi(3, x0), g_ao(0, x1), g_wo(0, o0), g_bo(o1), g_wo(1, x0), g_ao(1, x1),
            g_wo(2, o0), g_wo(3, o1), g_bi(0, x0), g_bi(1, x1))}
        before, last_in = {}, {}
        for name in ORDER:
            key = G[name]["bank"].name
            before[name] = last_in.get(key)
            last_in[key] = name

        def spread(copy, to, src, blocks, every=R, at=0):
            to = to.rearrange("p j (i c) -> p j i c", c=every)[:, :, :, at:at + R]
            return copy(to, src.unsqueeze(2).broadcast_to([P, src.shape[1], blocks, R]))

        def spread_ai(copy, b, at, src):
            hi, lo = (src(s).bitcast(F32) for s in (HI, LO))
            spread(copy, ai_stack[:, b, :, 0:3 * BLK], hi, 3, BLK, at)
            return copy(ai_stack[:, b, :, 3 * BLK + at:3 * BLK + at + R], lo)

        block = ctx.enter_context(nc.Block())

        @block.sync
        def _(sp):
            x_rows = x_nat[:, :, :].rearrange("p (b u) d -> p b (u d)", b=PAIR)
            sp.dma_start(x_rows[:, 0, :], xv[0, 0]).then_inc(x_in[0], 16)
            sp.dma_start(idt[:, :], ids.rearrange("(o n) -> o n", o=1)).then_inc(ids_in, 16)
            sp.dma_start(ai_nat[:, :], e_wi_a.rearrange("e r d -> (e r) d")).then_inc(ai_in, 16)
            sp.dma_start(aic_nat[:, :], c_wi_a).then_inc(ai_in, 16)
            sp.dma_start(bic_nat[:, :, :], c_wi_b.rearrange("(p j) r -> p j r", p=P)).then_inc(bic_in, 16)
            sp.wait_ge(ids_in, 16)
            first = [sp.value_load(idt[0:1, b:b + 1], min_val=0, max_val=E - 1) for b in range(PAIR)]
            for b in range(PAIR):
                sp.dma_start(bi0_raw[:, b, :, :], e_wi_b[bass.ds(first[b], 1), :, :].rearrange("o (p j) r -> (o p) j r", p=P)
                             ).then_inc(bi0_in[b], 16)
            sp.dma_start(boc_nat[:, :, :], c_wo_b.rearrange("(p k) r -> p k r", p=P)).then_inc(boc_in, 16)
            sp.dma_start(wi_nat[:, 4:, :], wi.rearrange("(j p) d -> p j d", p=P)[:, 4:, :]).then_inc(wi_in[2], 16)
            for i in range(3):
                sp.dma_start(aoc_nat[i * R:(i + 1) * R, :], c_wo_a).then_inc(aoc_in, 16)
            sp.dma_start(wo_nat[:, :, :], wo.rearrange("(k p) f -> p k f", p=P)).then_inc(wo_in, 16)
            sp.dma_start(ao_nat[:, :], e_wo_a.rearrange("e r f -> (e r) f")).then_inc(ao_in, 16)
            sp.dma_start(bo_raw[:, :, :], e_wo_b.rearrange("e (p k) r -> p e (k r)", p=P)).then_inc(bo_in, 16)
            sp.dma_start(bi_raw[:, :, :], e_wi_b.rearrange("e (p j) r -> p e (j r)", p=P)).then_inc(bi_in, 16)

            def expert_rows(step):
                rows = []
                for b in range(PAIR):
                    at = step * PAIR + b
                    at = slice(at, at + 1) if isinstance(step, int) else bass.ds(at, 1)
                    e = sp.value_load(idt[0:1, at], min_val=0, max_val=E - 1)
                    rows.append(sp.snap(e * R))
                return rows

            def load_bi(rows):
                for b in range(PAIR):
                    for i, s in enumerate(B_PART):
                        sp.dma_start(bi_stack[i * BLK:i * BLK + R, b, :].bitcast(F32),
                                     bi_parts[s, bass.ds(rows[b], R), :]).then_inc(bi_loaded, 16)

            def load_bo(rows, b):
                for i, s in enumerate(BO_PART):
                    at = i * R
                    sp.dma_start(bo_stack[at:at + R, b, :].bitcast(F32),
                                 bo_parts[s, bass.ds(rows[b], R), :]).then_inc(bo_loaded[b], 16)

            def store(step, t):
                sp.wait_ge(added, step * TT + t + 1)
                at = step if isinstance(step, int) else bass.ds(step, 1)
                to = ov[at, t // SEQ_TILES, t % SEQ_TILES, :, :]
                sp.dma_start(to if isinstance(step, int) else to.rearrange("o p d -> (o p) d"),
                             o_sb[:, t, :]).then_inc(stored, 16)

            def load_x(step):
                sp.wait_ge(xt_done, step * KD)
                sp.wait_ge(res_ready, step)
                for b in range(PAIR):
                    to = xv[step, b] if isinstance(step, int) else xv[bass.ds(step, 1), b, :, :].rearrange("o p n -> (o p) n")
                    sp.dma_start(x_rows[:, b, :], to).then_inc(x_in[b], 16)

            def step_io(q, more):
                rows = expert_rows(q + 1)
                after = sp.snap(q + 2) if more else None
                sp.wait_ge(up_done, (q + 1) * MF)
                sp.wait_ge(bi_out, 32)
                load_bi(rows)
                store(q, 0)
                store(q, 1)
                sp.wait_ge(fin_done, q * TT + 2)
                load_bo(rows, 0)
                store(q, 2)
                store(q, 3)
                sp.wait_ge(fin_done, q * TT + 4)
                load_bo(rows, 1)
                if more:
                    load_x(after)

            load_x(1)
            sp.wait_ge(wt_out, OUT["bo"])
            for s in (HI, LO):
                sp.dma_start(bo_parts[s], boT[s][:, :].bitcast(F32)).then_inc(bo_out, 16)
            sp.wait_ge(bo_out, 32)
            rows = expert_rows(0)
            for b in range(PAIR):
                load_bo(rows, b)

            with sp.Fori(0, STEPS - 2) as q:
                step_io(q, True)
            step_io(STEPS - 2, False)
            for t in range(TT):
                store(STEPS - 1, t)
            sp.wait_ge(stored, STEPS * TT * 16)

        @block.gpsimd
        def _(pool):
            nc.gpsimd.memset(ident[:, :], 0.0).then_inc(ident_zero, 1)
            pool.wait_ge(ident_zero, 1)
            nc.gpsimd.affine_select(out=ident[:, :], in_=ident[:, :], compare_op=ALU.not_equal, fill=1.0, base=0,
                                    pattern=[[-1, P]], channel_multiplier=1).then_inc(ident_ready, 1)

            def experts(step):
                return [pool.value_load(idt[0:1, bass.ds(step * PAIR + b, 1)], min_val=0, max_val=E - 1)
                        for b in range(PAIR)]

            def copy_ai(at):
                for b in range(PAIR):
                    last = spread_ai(nc.gpsimd.tensor_copy, b, 0, lambda s: aiT[s][:, 0:KD * ER].rearrange("p (k n) -> p k n", k=KD)[
                        :, :, bass.ds(at[b], R)])
                last.then_inc(ai_ready, 1)

            def copy_ao(at, b):
                to = [0, R + D][b]
                for s in (HI, LO):
                    last = nc.gpsimd.tensor_copy(wcat[s][:, :, to:to + R], aoT[s][:, :, bass.ds(at[b], R)].bitcast(F32))
                last.then_inc(ao_ready[b], 1)

            pool.wait_ge(ids_in, 16)
            at = [pool.snap(e * R) for e in experts(0)]
            pool.wait_ge(wt_out, OUT["ai"])
            copy_ai(at)
            pool.wait_ge(boc_in, 16)
            spread(nc.gpsimd.tensor_copy, boc0_nat[:, :, :], boc_nat[:, :, :], 3).then_inc(nat_ready, 1)
            pool.wait_ge(aoc_in, 3 * 16)
            nc.gpsimd.tensor_copy(aoc_stack[:, :], aoc_nat[:, :]).then_inc(aoc_hi, 1)
            pool.wait_ge(aoc_hi, 1)
            rows = aoc_stack[TL_LO:KL, :]
            nc.gpsimd.tensor_tensor(rows, aoc_nat[TL_LO:KL, :], rows.bitcast(F32), ALU.subtract).then_inc(aoc_lo, 1)
            pool.wait_ge(aoc_lo, 1)
            pool.wait_ge(bo_in, 16)
            nc.gpsimd.tensor_copy(bo_nat[:, :, :].rearrange("p k (e r) -> p k e r", r=R),
                                  bo_raw[:, :, :].rearrange("p e (k r) -> p k e r", r=R)).then_inc(nat_ready, 1)
            pool.wait_ge(bi_in, 16)
            nc.gpsimd.tensor_copy(bi_nat[:, :, :].rearrange("p j (e r) -> p j e r", r=R),
                                  bi_raw[:, :, :].rearrange("p e (j r) -> p j e r", r=R)).then_inc(nat_ready, 1)
            pool.wait_ge(wt_out, OUT["ao1"])
            for b in range(PAIR):
                copy_ao(at, b)
            with pool.Fori(0, STEPS - 1) as q:
                at = [pool.snap(e * R) for e in experts(q + 1)]
                pool.wait_ge(low_done, q + 1)
                copy_ai(at)
                pool.wait_ge(main_done, q * TT + 2)
                copy_ao(at, 0)
                pool.wait_ge(main_done, q * TT + 4)
                copy_ao(at, 1)

        @block.scalar
        def _(act):
            wi_rows = wi.rearrange("(j p) d -> p j d", p=P)
            act.dma_start(wi_nat[:, 0:2, :], wi_rows[:, 0:2, :]).then_inc(wi_in[0], 16)
            act.dma_start(x_nat[:, SEQ_TILES:, :].rearrange("p u d -> p (u d)"), xv[0, 1]).then_inc(x_in[1], 16)
            act.wait_ge(zeros_ready, 1)
            nc.scalar.copy(act_warm[:, :], zeros[:, 0:1])
            act.dma_start(wi_nat[:, 2:4, :], wi_rows[:, 2:4, :]).then_inc(wi_in[1], 16)

            def group_hi(name):
                g = G[name]
                act.wait_ge(wt_done, OUT[name])
                for out_, src, scale in g["hi"]:
                    last = nc.scalar.copy(out_, src) if scale is None else nc.scalar.mul(out_, src, scale)
                last.then_inc(wt_hi, 1)

            def copy_bi0(b):
                act.wait_ge(bi0_in[b], 16)
                spread(nc.scalar.copy, bi0_nat[:, b, :, :], bi0_raw[:, b, :, :], 4, BLK).then_inc(bi0_expert, 1)

            def x_hi(step):
                for k in range(KD):
                    act.wait_ge(xt_done, step * KD + k + 1)
                    nc.scalar.copy(xT[HI][:, k, :], bank_x[k][:, :]).then_inc(xt_hi, 1)

            def lowi_hi(step):
                act.wait_ge(low_done, step + 1)
                nc.scalar.mul(low_stack[:, :], bank_x[0][:, :], ALPHA).then_inc(low_hi, 1)

            def hidden_hi(step, m):
                act.wait_ge(up_done, step * MF + m + 1)
                nc.scalar.activation(hid[HI][:, m, :], bank_h[m % 4][:, :], ACT.Relu).then_inc(hid_hi, 1)

            def low_copy(step, t):
                act.wait_ge(main_done, step * TT + t + 1)
                at = RANK_AT[t // SEQ_TILES]
                ranks = out_bank[t][:, at:at + R]
                nc.scalar.copy(lo_sb[t % 2][:, :, :], ranks.unsqueeze(1).broadcast_to([P, P // R, R])).then_inc(lo_copied, 1)

            def tl_part(step, t):
                act.wait_ge(tl_done, step * TT + t + 1)
                nc.scalar.mul(lo_stack[t % 2][:, :], tl_bank[t][0:KL, 0:P], ALPHA).then_inc(tl_hi, 1)

            def down(step, more):
                low_copy(step, 0)
                tl_part(step, 0)
                if more:
                    x_hi(step + 1)
                low_copy(step, 1)
                tl_part(step, 1)
                low_copy(step, 2)
                tl_part(step, 2)
                low_copy(step, 3)
                tl_part(step, 3)
                if more:
                    lowi_hi(step + 1)

            for what in FIRST:
                if isinstance(what, str):
                    group_hi(what)
                    if what == "ai":
                        copy_bi0(0)
                        act.wait_ge(wt_out, OUT["ai"])
                        for b in range(PAIR):
                            last = spread_ai(nc.scalar.copy, b, R,
                                             lambda s: aiT[s][:, KD * ER:].rearrange("p (k n) -> p k n", k=KD))
                        last.then_inc(common_ready, 1)
                        copy_bi0(1)
                elif what[0] == "x":
                    x_hi(0)
                elif what[0] == "low":
                    lowi_hi(0)
                elif what[0] == "lora":
                    hidden_hi(0, what[1])
            act.wait_ge(wt_out, OUT["bi1"])
            for s in (HI, LO):
                act.dma_start(bi_parts[s], biT[s][:, :].bitcast(F32)).then_inc(bi_out, 16)

            with act.Fori(0, STEPS - 1) as q:
                down(q, True)
                for m in range(MF):
                    hidden_hi(q + 1, m)
            down(STEPS - 1, False)

        @block.vector
        def _(dve):
            def lo_part(out_, src, scale, hi):
                op = ALU.max if scale is None else ALU.mult
                return nc.vector.scalar_tensor_tensor(out=out_, in0=src, scalar=0.0 if scale is None else scale,
                                                      in1=hi.bitcast(F32), op0=op, op1=ALU.subtract)

            def group_out(name):
                g = G[name]
                dve.wait_ge(wt_hi, OUT[name])
                for out_, src, hi, scale in g["lo"]:
                    last = (nc.vector.tensor_tensor(out_, src, hi.bitcast(F32), ALU.subtract) if scale is None
                            else lo_part(out_, src, scale, hi))
                last.then_inc(wt_out, 1)

            def x_lo(step):
                for k in range(KD):
                    dve.wait_ge(xt_hi, step * KD + k + 1)
                    nc.vector.tensor_tensor(xT[LO][:, k, :], bank_x[k][:, :], xT[HI][:, k, :].bitcast(F32),
                                            ALU.subtract).then_inc(xt_lo, 1)

            def keep_x(step):
                for b in range(PAIR):
                    dve.wait_ge(x_in[b], (step + 1) * 16)
                if not isinstance(step, int):
                    dve.wait_ge(added, step * TT)
                nc.vector.tensor_copy(x_res[:, :, :], x_nat[:, :, :]).then_inc(res_ready, 1)

            def lowi_lo(step):
                dve.wait_ge(low_hi, step + 1)
                rows = low_stack[LOW_LO:LOW_LO + BLK, :]
                lo_part(rows, bank_x[0][LOW_LO:LOW_LO + BLK, :], ALPHA, rows).then_inc(low_lo, 1)

            def hidden_lo(step, m):
                dve.wait_ge(hid_hi, step * MF + m + 1)
                lo_part(hid[LO][:, m, :], bank_h[m % 4][:, :], None, hid[HI][:, m, :]).then_inc(hid_lo, 1)

            def tl_lo_part(step, t):
                dve.wait_ge(tl_hi, step * TT + t + 1)
                rows = lo_stack[t % 2][TL_LO:KL, :]
                lo_part(rows, tl_bank[t][TL_LO:KL, 0:P], ALPHA, rows).then_inc(tl_lo, 1)

            def add(step, t):
                b = t // SEQ_TILES
                dve.wait_ge(fin_done, step * TT + t + 1)
                if t == 0:
                    dve.wait_ge(res_ready, step + 1)
                    dve.wait_ge(stored, step * TT * 16)
                nc.vector.tensor_tensor(o_sb[:, t, :], out_bank[t][:, OUT_AT[b]:OUT_AT[b] + D], x_res[:, t, :],
                                        ALU.add).then_inc(added, 1)

            def down(step, more):
                tl_lo_part(step, 0)
                if more:
                    x_lo(step + 1)
                add(step, 0)
                tl_lo_part(step, 1)
                add(step, 1)
                tl_lo_part(step, 2)
                add(step, 2)
                tl_lo_part(step, 3)
                if more:
                    lowi_lo(step + 1)
                add(step, 3)
                if more:
                    keep_x(step + 1)

            nc.vector.memset(zeros[:, :], 0.0).then_inc(zeros_ready, 1)
            for what in FIRST:
                if isinstance(what, str):
                    group_out(what)
                    if what == "ai":
                        dve.wait_ge(bic_in, 16)
                        for b in range(PAIR):
                            spread(nc.vector.tensor_copy, bi0_nat[:, b, :, :], bic_nat[:, :, :], 4, BLK, R).then_inc(bi0_common, 1)
                    if what == "bi011":
                        keep_x(0)
                elif what[0] == "x":
                    x_lo(0)
                elif what[0] == "low":
                    lowi_lo(0)
                elif what[0] == "lora":
                    hidden_lo(0, what[1])
            with dve.Fori(0, STEPS - 1) as q:
                down(q, True)
                for m in range(MF):
                    hidden_lo(q + 1, m)
            down(STEPS - 1, False)

        @block.tensor
        def _(pe):
            def run_group(name):
                g = G[name]
                for s, v in g["wait"]:
                    pe.wait_ge(s, v)
                if before[name]:
                    pe.wait_ge(wt_out, OUT[before[name]])
                for i, (dst, src) in enumerate(g["tiles"]):
                    last = nc.tensor.matmul(dst, src, ident[0:src.shape[0], 0:src.shape[0]], is_transpose=True,
                                            start=(i == 0), stop=(not g["products"] and i == len(g["tiles"]) - 1))
                for i, (dst, lhsT, rhs) in enumerate(g["products"]):
                    last = nc.tensor.matmul(dst, lhsT, rhs, start=False, stop=(i == len(g["products"]) - 1))
                last.then_inc(wt_done, 1)

            def transpose_x(step, k, b):
                pe.wait_ge(x_in[b], (step + 1) * 16)
                for t in range(b * SEQ_TILES, (b + 1) * SEQ_TILES):
                    last = nc.tensor.transpose(bank_x[k][:, t * P:(t + 1) * P], x_nat[:, t, k * P:(k + 1) * P],
                                               ident[:, :])
                if b == PAIR - 1:
                    last.then_inc(xt_done, 1)

            def low_in(step, b):
                if b == 0:
                    pe.wait_ge(xt_lo, (step + 1) * KD)
                    pe.wait_ge(ai_ready, step + 1)
                cols = slice(b * S, (b + 1) * S)
                for k in range(KD):
                    for s in (HI, LO):
                        last = nc.tensor.matmul(bank_x[0][:, cols], ai_stack[:, b, k, :], xT[s][:, k, cols],
                                                start=(k == 0 and s == HI), stop=(k == KD - 1 and s == LO))
                if b == PAIR - 1:
                    last.then_inc(low_done, 1)

            def up_main(step, m):
                if m >= 4:
                    pe.wait_ge(hid_lo, step * MF + m - 3)
                f = slice(m * P, (m + 1) * P)
                for i, (sw, sx, k) in enumerate((sw, sx, k) for sw, sx in ((HI, HI), (LO, HI), (HI, LO))
                                                for k in range(KD)):
                    if isinstance(step, int) and m == 0:
                        if sw == LO:
                            pe.wait_ge(wt_out, OUT["wi0"])
                        elif sx == HI:
                            pe.wait_ge(xt_hi, k + 1)
                        else:
                            pe.wait_ge(xt_lo, k + 1)
                    nc.tensor.matmul(bank_h[m % 4][:, :], wiT[sw][:, k, f], xT[sx][:, k, :], start=(i == 0), stop=False)

            def up_lora(step, m):
                if m == 0:
                    pe.wait_ge(low_lo, step + 1)
                    if isinstance(step, int):
                        pe.wait_ge(wt_out, OUT["bi011"])
                    else:
                        pe.wait_ge(bi_loaded, step * PAIR * 4 * 16)
                for b in range(PAIR):
                    cols = slice(b * S, (b + 1) * S)
                    last = nc.tensor.matmul(bank_h[m % 4][:, cols], bi_stack[:, b, m * P:(m + 1) * P],
                                            low_stack[:, cols], start=False, stop=(b == PAIR - 1))
                last.then_inc(up_done, 1)

            def up(step):
                for m in range(1, MF + 1):
                    if m < MF:
                        up_main(step, m)
                    up_lora(step, m - 1)

            def first_up():
                for what in FIRST:
                    if isinstance(what, str):
                        if what == "bi000":
                            pe.wait_ge(xt_lo, KD)
                        if what == "wi3":
                            pe.wait_ge(low_lo, 1)
                        run_group(what)
                    elif what[0] == "x":
                        for k in range(KD):
                            transpose_x(0, k, 1)
                    elif what[0] == "low":
                        pe.wait_ge(common_ready, 1)
                        low_in(0, 0)
                        low_in(0, 1)
                    elif what[0] == "lora":
                        up_lora(0, what[1])
                    else:
                        m = what[1]
                        if m in (2, 4, 6):
                            pe.wait_ge(wt_out, OUT[f"wi{m // 2}"])
                        if m == 3:
                            pe.wait_ge(wt_out, OUT["ai"])
                        up_main(0, m)

            def main(step, t, tiles=range(MF)):
                b = t // SEQ_TILES
                tok = slice(t * P, (t + 1) * P)
                win = slice(WIN_AT[b], WIN_AT[b] + WIN)
                if 0 in tiles:
                    if t % SEQ_TILES == 0:
                        pe.wait_ge(ao_ready[b], step + 1)
                    if t == 1:
                        pe.wait_ge(hid_lo, step * MF + 6)
                    if t == 2:
                        pe.wait_ge(wt_out, OUT[ORDER[-1]])
                        pe.wait_ge(added, step * TT)
                for m in tiles:
                    if t == 0:
                        pe.wait_ge(hid_lo, step * MF + max(m + 1, 5))
                    for i, (sh, sw) in enumerate(((HI, HI), (HI, LO), (LO, HI))):
                        last = nc.tensor.matmul(out_bank[t][:, 0:WIN], hid[sh][:, m, tok], wcat[sw][:, m, win],
                                                start=(m == 0 and i == 0), stop=(m == MF - 1 and i == 2))
                if MF - 1 in tiles:
                    last.then_inc(main_done, 1)

            def turn_low(step, t):
                pe.wait_ge(lo_copied, step * TT + t + 1)
                if t < 2:
                    pe.wait_ge(hid_lo, step * MF + 7 + t)
                nc.tensor.transpose(tl_bank[t][:, 0:P], lo_sb[t % 2][:, :, :].rearrange("p i r -> p (i r)"),
                                    ident[:, :]).then_inc(tl_done, 1)

            def fin(step, t):
                b = t // SEQ_TILES
                pe.wait_ge(tl_lo, step * TT + t + 1)
                if t % SEQ_TILES == 0:
                    pe.wait_ge(bo_loaded[b], (step + 1) * 3 * 16)
                nc.tensor.matmul(out_bank[t][:, OUT_AT[b]:OUT_AT[b] + D], lo_stack[t % 2][:, :], bo_stack[:, b, :],
                                 start=False, stop=True, skip_group_check=True).then_inc(fin_done, 1)

            def down(step, more):
                main(step, 0)
                main(step, 1)
                turn_low(step, 0)
                if more:
                    pe.wait_ge(wt_out, OUT[ORDER[-1]])
                    for k in range(KD):
                        for b in range(PAIR):
                            transpose_x(step + 1, k, b)
                main(step, 2, FIRST_HALF)
                fin(step, 0)
                turn_low(step, 1)
                main(step, 2, SECOND_HALF)
                main(step, 3, FIRST_HALF)
                fin(step, 1)
                turn_low(step, 2)
                main(step, 3, SECOND_HALF)
                fin(step, 2)
                if more:
                    low_in(step + 1, 0)
                turn_low(step, 3)
                if more:
                    low_in(step + 1, 1)
                    up_main(step + 1, 0)
                fin(step, 3)

            pe.wait_ge(zeros_ready, 1)
            for _ in range(WARM_UP):
                nc.tensor.matmul(bank_h[0][:, 0:P], zeros[:, :], zeros[:, :], start=True, stop=True)
            pe.wait_ge(ident_ready, 1)
            for k in range(KD):
                transpose_x(0, k, 0)
            first_up()
            pe.wait_ge(wt_out, OUT["wo3"])
            with pe.Fori(0, STEPS - 1) as q:
                down(q, True)
                up(q + 1)
            down(STEPS - 1, False)


_INS = ["x", "itok_B_0_7", "L0_cond_wi", "L0_cond_wo", "L0_cond_common_wi_a", "L0_cond_common_wi_b",
        "L0_cond_common_wo_a", "L0_cond_common_wo_b", "L0_cond_experts_wi_a", "L0_cond_experts_wi_b",
        "L0_cond_experts_wo_a", "L0_cond_experts_wo_b"]


def kernel(**inputs):
    import numpy as np
    import concourse.bacc as bacc
    from concourse.bass_utils import run_bass_kernel_spmd

    nc = bacc.Bacc("TRN2", target_bir_lowering=False, num_devices=1)
    arrays, args = {}, []
    for name in _INS:
        a = np.ascontiguousarray(inputs[name])
        arrays[f"in_{name}"] = a
        args.append(nc.dram_tensor(f"in_{name}", a.shape, mybir.dt.from_np(a.dtype), kind="ExternalInput").ap())
    args.append(nc.dram_tensor("out_0", inputs["x"].shape, F32, kind="ExternalOutput").ap())
    conditional_ffn(nc, *args)
    result = run_bass_kernel_spmd(nc, [arrays], core_ids=[0])
    return result.results[0]["out_0"]
```
